# Optimizing a Trainium2 kernel written in Bass

```python
import numpy as np
import jax
import jax.numpy as jnp

def _softmax(x, axis=-1):
    return jax.nn.softmax(x, axis=axis)

def _gelu(x):
    return jax.nn.gelu(x, approximate=True)

def _silu(x):
    return jax.nn.silu(x)

def _sigmoid(x):
    return jax.nn.sigmoid(x)

def _layernorm(x, axis=-1, eps=1e-05):
    m = jnp.mean(x, axis=axis, keepdims=True)
    v = jnp.var(x, axis=axis, keepdims=True)
    return (x - m) / jnp.sqrt(v + eps)

def _scatter_add(tgt, idx, src, axis=0):
    return tgt.at[idx].add(src)

def _segment_sum(src, seg, n):
    return jax.ops.segment_sum(src, seg, n)
kernel_name = 'mk_adaln_d1_jaxref_r8_ee359a'

def setup_inputs(seed: int=0):
    np.random.seed(seed)
    _w = jnp.asarray

    def _L0_attn_setup():
        import jax, jax.numpy as jnp
        import numpy as np
        HIDDEN = 512
        NHQ = 32
        NHKV = 8
        HEAD_DIM = HIDDEN // NHQ
        THETA = 10000.0

        def _rope(x, theta_base):
            b, h, s, d = x.shape
            inv_freq = 1.0 / theta_base ** (jnp.arange(0, d, 2, dtype=jnp.float32)[:d // 2] / d)
            freqs = jnp.arange(s, dtype=jnp.float32)[:, None] * inv_freq[None, :]
            cos = jnp.cos(freqs).astype(x.dtype)
            sin = jnp.sin(freqs).astype(x.dtype)
            x1, x2 = (x[..., :d // 2], x[..., d // 2:])
            return jnp.concatenate([x1 * cos - x2 * sin, x2 * cos + x1 * sin], axis=-1)
        key = jax.random.key(seed)
        ks = jax.random.split(key, 5)
        std = 1.0 / np.sqrt(HIDDEN)
        x = jax.random.normal(ks[0], (2, 256, HIDDEN), dtype=jnp.float32)
        Wq = jax.random.normal(ks[1], (HIDDEN, HIDDEN), dtype=jnp.float32) * std
        Wk = jax.random.normal(ks[2], (HIDDEN, NHKV * HEAD_DIM), dtype=jnp.float32) * std
        Wv = jax.random.normal(ks[3], (HIDDEN, NHKV * HEAD_DIM), dtype=jnp.float32) * std
        Wo = jax.random.normal(ks[4], (HIDDEN, HIDDEN), dtype=jnp.float32) * std
        return {'x': x, 'Wq': Wq, 'Wk': Wk, 'Wv': Wv, 'Wo': Wo}
    _L0_attn_in = _L0_attn_setup()

    def _L0_ffn_setup():
        import jax, jax.numpy as jnp
        import numpy as np
        M = 512
        K = 512

        def _make_2to4_mask(key, shape):
            scores = jax.random.normal(key, shape)
            g = scores.reshape(shape[0], shape[1] // 4, 4)
            rank = jnp.argsort(jnp.argsort(-jnp.abs(g), axis=-1), axis=-1)
            return (rank < 2).reshape(shape).astype(jnp.float32)
        key = jax.random.key(seed)
        k_x, k_w12, k_b12, k_w3, k_b3, k_m = jax.random.split(key, 6)
        x = jax.random.normal(k_x, (4, 256, K), dtype=jnp.float32)
        w12_dense = jax.random.normal(k_w12, (2 * M, K), dtype=jnp.float32) * (1.0 / np.sqrt(K))
        mask12 = _make_2to4_mask(k_m, (2 * M, K))
        w12 = w12_dense * mask12
        b12 = jax.random.normal(k_b12, (2 * M,), dtype=jnp.float32) * 0.01
        w3 = jax.random.normal(k_w3, (M, M), dtype=jnp.float32) * (1.0 / np.sqrt(M))
        b3 = jax.random.normal(k_b3, (M,), dtype=jnp.float32) * 0.01
        return {'x': x, 'w12': w12, 'b12': b12, 'w3': w3, 'b3': b3}
    _L0_ffn_in = _L0_ffn_setup()
    _L0_c = _w((lambda *s: np.random.randn(*s).astype(np.float32) * 0.05)(4, 512))
    _L0_wmod = _w((lambda *s: np.random.randn(*s).astype(np.float32) * 0.05)(512, 6 * 512) * 512 ** (-0.5))
    _d = {'L0_attn_x': _L0_attn_in['x'], 'L0_attn_Wq': _L0_attn_in['Wq'], 'L0_attn_Wk': _L0_attn_in['Wk'], 'L0_attn_Wv': _L0_attn_in['Wv'], 'L0_attn_Wo': _L0_attn_in['Wo'], 'L0_ffn_w12': _L0_ffn_in['w12'], 'L0_ffn_b12': _L0_ffn_in['b12'], 'L0_ffn_w3': _L0_ffn_in['w3'], 'L0_ffn_b3': _L0_ffn_in['b3'], 'L0_c': _L0_c, 'L0_wmod': _L0_wmod}
    _x0 = _d['L0_attn_x']
    _d['L0_attn_x'] = jax.random.normal(jax.random.fold_in(jax.random.key(seed), 1), (4, 256, 512), dtype=_x0.dtype)
    del _x0
    return _d

def reference(L0_attn_x, L0_attn_Wq, L0_attn_Wk, L0_attn_Wv, L0_attn_Wo, L0_ffn_w12, L0_ffn_b12, L0_ffn_w3, L0_ffn_b3, L0_c, L0_wmod):

    def _L0_attn_ref(x, Wq, Wk, Wv, Wo):
        import jax, jax.numpy as jnp
        import numpy as np
        HIDDEN = 512
        NHQ = 32
        NHKV = 8
        HEAD_DIM = HIDDEN // NHQ
        THETA = 10000.0

        def _rope(x, theta_base):
            b, h, s, d = x.shape
            inv_freq = 1.0 / theta_base ** (jnp.arange(0, d, 2, dtype=jnp.float32)[:d // 2] / d)
            freqs = jnp.arange(s, dtype=jnp.float32)[:, None] * inv_freq[None, :]
            cos = jnp.cos(freqs).astype(x.dtype)
            sin = jnp.sin(freqs).astype(x.dtype)
            x1, x2 = (x[..., :d // 2], x[..., d // 2:])
            return jnp.concatenate([x1 * cos - x2 * sin, x2 * cos + x1 * sin], axis=-1)
        b, s, _ = x.shape
        q_per_kv = NHQ // NHKV
        q = (x @ Wq).reshape(b, s, NHQ, HEAD_DIM).transpose(0, 2, 1, 3)
        k = (x @ Wk).reshape(b, s, NHKV, HEAD_DIM).transpose(0, 2, 1, 3)
        v = (x @ Wv).reshape(b, s, NHKV, HEAD_DIM).transpose(0, 2, 1, 3)
        q = _rope(q, THETA)
        k = _rope(k, THETA)
        qg = q.reshape(b, NHKV, q_per_kv, s, HEAD_DIM)
        scores = jnp.einsum('bkgqd,bkmd->bkgqm', qg, k) / np.sqrt(HEAD_DIM)
        causal = jnp.tril(jnp.ones((s, s), dtype=bool))
        scores = jnp.where(causal, scores, -jnp.inf)
        attn = jax.nn.softmax(scores, axis=-1)
        out = jnp.einsum('bkgqm,bkmd->bkgqd', attn, v)
        out = out.reshape(b, NHQ, s, HEAD_DIM).transpose(0, 2, 1, 3).reshape(b, s, HIDDEN)
        return out @ Wo

    def _L0_ffn_ref(x, w12, b12, w3, b3):
        import jax, jax.numpy as jnp
        import numpy as np
        M = 512
        K = 512

        def _make_2to4_mask(key, shape):
            scores = jax.random.normal(key, shape)
            g = scores.reshape(shape[0], shape[1] // 4, 4)
            rank = jnp.argsort(jnp.argsort(-jnp.abs(g), axis=-1), axis=-1)
            return (rank < 2).reshape(shape).astype(jnp.float32)
        x12 = jnp.einsum('bsk,mk->bsm', x, w12) + b12
        x1, x2 = jnp.split(x12, 2, axis=-1)
        x4 = jax.nn.silu(x1) * x2
        return jnp.einsum('bsm,nm->bsn', x4, w3) + b3
    x = L0_attn_x
    mod = (_silu(L0_c) @ L0_wmod).reshape(L0_c.shape[0], 6, 1, -1)
    sa, ca, ga, sb, cb, gb = (mod[:, 0], mod[:, 1], mod[:, 2], mod[:, 3], mod[:, 4], mod[:, 5])
    ga = (2 * (ga >= 0) - 1) * jnp.maximum(jnp.abs(ga), 0.25)
    gb = (2 * (gb >= 0) - 1) * jnp.maximum(jnp.abs(gb), 0.25)
    h = _layernorm(x, axis=-1) * (1 + ca) + sa
    x = x + ga * _L0_attn_ref(h, L0_attn_Wq, L0_attn_Wk, L0_attn_Wv, L0_attn_Wo)
    h = _layernorm(x, axis=-1) * (1 + cb) + sb
    x = x + gb * _L0_ffn_ref(h, L0_ffn_w12, L0_ffn_b12, L0_ffn_w3, L0_ffn_b3)
    return x

_drawn_inputs = setup_inputs


def setup_inputs(seed=0):
    import zlib

    import numpy as np

    out = dict(_drawn_inputs(seed))
    spreads = {}
    factors = {'L0_ffn_b12': 31.453, 'L0_ffn_b3': 23.24}
    for name, (base, spread) in spreads.items():
        noise = np.random.default_rng([zlib.crc32(name.encode()), seed]).standard_normal(out[name].shape)
        drawn = base * np.exp(spread * noise) if base else spread * noise
        out[name] = jnp.asarray(drawn.astype(out[name].dtype))
    for name, factor in factors.items():
        out[name] = (out[name] * factor).astype(out[name].dtype)
    return out
```

```python
import numpy as np
from contextlib import ExitStack
import concourse.bass as bass
from concourse import mybir

B, S, D = 4, 256, 512
P = 128
DH = 16
NKV, G = 8, 4
KC = D // P
NT = S // P
M = 512
MC = M // P
NJ, NH = 4, 2
EPS = 1e-5
NEG = -3.0e38
GATE_MIN = 0.25
NPIECE = 3

UNITS = [(qt, h, kt) for qt in range(NT) for h in range(NH) for kt in range(qt + 1)]
NU = len(UNITS)
MASKED = [qt == kt for qt, h, kt in UNITS]


def make_schedule():
    s = [("mods", 0, 0), ("ln", 1, 0), ("modt", 0, 0), ("tr", 1, 0, 0), ("tr", 1, 0, 1)]
    s += [("qk", 0, i) for i in range(3)]
    s += [("ln", 1, 1), ("tr", 1, 1, 0), ("tr", 1, 1, 1)]
    for b in range(B + 1):
        now, prev, nxt = b < B, b >= 1, b + 1 < B
        def at(ok, *stage):
            if ok:
                s.append(stage)
        at(now, "max", b, 0)
        at(prev, "wo", b - 1, 1)
        at(prev, "ln", 2, b - 1)
        at(now, "max", b, 1)
        at(nxt, "qk", b + 1, 0)
        at(now, "max", b, 2)
        at(nxt, "qk", b + 1, 1)
        at(now, "max", b, 3)
        at(nxt, "qk", b + 1, 2)
        at(b == 0, "mods", 1, 0)
        at(b == 0, "modt", 1, 0)
        at(b == 0, "mods", 2, 0)
        at(now, "max", b, 4)
        at(now, "mt", b, 0)
        at(prev, "tr", 2, b - 1, 0)
        at(prev, "tr", 2, b - 1, 1)
        at(now, "max", b, 5)
        at(prev, "up", b - 1, 0)
        at(now, "max", b, 6)
        at(prev, "up", b - 1, 1)
        at(now, "max", b, 7)
        at(prev, "up", b - 1, 2)
        at(prev, "up", b - 1, 3)
        at(now, "st", b, 0)
        at(now, "mt", b, 1)
        at(now, "st", b, 1)
        at(now, "pv", b, 0)
        at(prev, "down", b - 1, 0)
        at(now, "st", b, 2)
        at(now, "pv", b, 1)
        at(now, "norm", b, 0)
        at(prev, "down", b - 1, 1)
        at(now, "st", b, 3)
        at(now, "wo", b, 0)
        at(now, "pv", b, 2)
        at(b + 2 < B, "ln", 1, b + 2)
        at(now, "st", b, 4)
        at(now, "pv", b, 3)
        at(b + 2 < B, "tr", 1, b + 2, 0)
        at(now, "st", b, 5)
        at(now, "pv", b, 4)
        at(b + 2 < B, "tr", 1, b + 2, 1)
        at(now, "pv", b, 5)
        at(now, "norm", b, 1)
    return s


SCHEDULE = make_schedule()
KINDS = {e[0] for e in SCHEDULE}
NTH = {e: sum(1 for f in SCHEDULE[:n] if f[0] == e[0]) for n, e in enumerate(SCHEDULE)}
GEN_KINDS = ("mods", "modt", "tr", "qk", "mt", "wo", "up", "down")
GEN_ORDER = [e for e in SCHEDULE if e[0] in GEN_KINDS]
GEN = {e: n for n, e in enumerate(GEN_ORDER)}


def build(nc, x, c_t, wmod, wq, wk, wv, wo, w12, w3, b12, b3, rope, half_cols, ident, ident16, mask16, sel16, out):
    F32, BF16 = mybir.dt.float32, mybir.dt.bfloat16
    ALU, ACT, AX = mybir.AluOpType, mybir.ActivationFunctionType, mybir.AxisListType
    ctx = ExitStack()
    with ctx:
        def sb(name, shape, dt=F32):
            return ctx.enter_context(nc.sbuf_tensor(name, shape, dt))

        def ps(name, shape, dt=F32):
            return ctx.enter_context(nc.psum_tensor(name, shape, dt))

        def sem(name):
            return ctx.enter_context(nc.semaphore(name))

        x_sb = sb("x_sb", [P, B, NT, D])
        wmod_sb = sb("wmod_sb", [P, 6, KC, D])
        wq_sb = sb("wq_sb", [P, KC, G, P])
        wk_sb = sb("wk_sb", [P, KC, P])
        wv_sb = sb("wv_sb", [P, KC, P])
        wo_sb = sb("wo_sb", [P, G, D])
        w12_sb = wmod_sb[:, 0:2].rearrange("p s k n -> p (s k n)").rearrange("p (k n) -> p k n", k=KC)
        w3_sb = wmod_sb[:, 2]
        gb3_sb = wmod_sb[:, 3]
        b12_sb = sb("b12_sb", [P, 2 * MC])
        b3_sb = sb("b3_sb", [P, D])
        rope_sb = sb("rope_sb", [P, 2, S])
        half_sb = sb("half_sb", [P, NH])
        ident_sb = sb("ident_sb", [P, P])
        ident16_sb = sb("ident16_sb", [P, P], BF16)
        mask16_sb = sb("mask16_sb", [P, P], BF16)
        sel16_sb = sb("sel16_sb", [P, NH, P], BF16)
        c_sb = sb("c_sb", [P, KC, B])
        c_exp = sb("c_exp", [P, KC, B])
        c_silu = sb("c_silu", [P, KC, 32])
        modrow = sb("modrow", [64, 2, D])
        shift_sb = sb("shift_sb", [P, 2, KC, B])
        scale_sb = sb("scale_sb", [P, 2, KC, B])
        g_sign = sb("g_sign", [64, D])
        g_rows = sb("g_rows", [64, D])
        gate_sb = sb("gate_sb", [P, 2, B, D])
        eps_half = sb("eps_half", [P, NT])
        st6 = sb("st6", [P, NT, 6])
        mv = sb("mv", [P, 2, NT, 2])
        rstd = sb("rstd", [P, NT])
        xn = sb("xn", [P, 2, NT, D])
        h_t = [sb("h1_t", [P, KC, S]), sb("h2_t", [P, KC, S])]
        raw = sb("raw", [P, 2, 2 * S])
        shuf = sb("shuf", [P, 2, 2 * S])
        rcos = sb("rcos", [P, 2, 2 * S])
        krot = sb("krot", [P, S])
        q_rot = sb("q_rot", [P, 2, G, S])
        k_pad = sb("k_pad", [P, 2, NH, S])
        v_pad = sb("v_pad", [P, 2, NT, NH, NJ, 32])
        ones_pad = sb("ones_pad", [P, NH, 32])
        mx = sb("mx", [P, NT, G, 2 * NJ])
        mres = sb("mres", [P, 2, G, 2 * NJ])
        m3 = sb("m3", [P, NT, G, P], BF16)
        m_t = sb("m_t", [P, NT, G * P], BF16)
        probs = sb("probs", [P, 3, NJ, G * P])
        rsum = sb("rsum", [P, G * P])
        o_sb = sb("o_sb", [P, 2, G * P])
        gated = sb("gated", [P, 2, D])
        act_s = sb("act_s", [P, 2, S])
        a_t = sb("a_t", [P, MC, S])

        gate_dram = nc.dram_tensor("gate_dram", (2, B, D), F32, kind="Internal").ap()

        sc_ps = ps("sc_ps", [P, NJ, 512])
        ot_ps = ps("ot_ps", [P, 512])
        sum_ps = ps("sum_ps", [P, 512])
        gen_ps = [ps("gen0_ps", [P, 512]), ps("gen1_ps", [P, 512])]

        loads = ["c", "ident", "rope", "half", "bf", "wq", "wk", "wv", "wo", "w12", "w3", "b12", "b3"]
        got = {k: sem(f"got_{k}") for k in loads}
        got_x = [sem(f"got_x{b}") for b in range(B)]
        got_mod = [sem(f"got_mod{i}") for i in range(3)]
        gate_stored = sem("gate_stored")
        got_gate = sem("got_gate")
        stored = sem("stored")
        zeroed = sem("zeroed")
        silu_exp = sem("silu_exp")
        silu_step = sem("silu_step")
        gen_full = [sem("gen_full0"), sem("gen_full1")]
        mod_row = sem("mod_row")
        mod_ready = sem("mod_ready")
        gate_step = sem("gate_step")
        gb3_ready = sem("gb3_ready")
        bn_done = sem("bn_done")
        mv_ready = sem("mv_ready")
        rstd_step = sem("rstd_step")
        xn_ready = sem("xn_ready")
        h_ready = [sem("h1_ready"), sem("h2_ready")]
        raw_ready = sem("raw_ready")
        v_ready = sem("v_ready")
        shuf_ready = sem("shuf_ready")
        rsin_ready = sem("rsin_ready")
        rcos_ready = sem("rcos_ready")
        rot_ready = sem("rot_ready")
        qk_ready = sem("qk_ready")
        max_full = sem("max_full")
        max_done = sem("max_done")
        piece = sem("piece")
        mt_ready = sem("mt_ready")
        st_full = sem("st_full")
        exp_done = sem("exp_done")
        mask_done = sem("mask_done")
        pv_done = sem("pv_done")
        rsum_ready = sem("rsum_ready")
        o_ready = sem("o_ready")
        gated_ready = sem("gated_ready")
        x2_ready = sem("x2_ready")
        x2b_ready = sem("x2b_ready")
        act_ready = sem("act_ready")
        a_ready = sem("a_ready")
        out_ready = sem("out_ready")

        def gen(entry):
            n = GEN[entry]
            return gen_ps[n % 2], gen_full[n % 2], n // 2

        def ngated(entry):
            return sum(1 for f in SCHEDULE[:SCHEDULE.index(entry)] if f[0] in ("wo", "down"))

        def read_out(entry):
            kind, n = entry[0], NTH[entry]
            if kind == "mods":
                return (mod_row, entry[1] + 1) if entry[1] < 2 else (gate_step, 4)
            if kind == "modt":
                return mod_ready, 2 * (n + 1)
            if kind == "tr":
                return h_ready[entry[1] - 1], KC * entry[2] + 2 * (entry[3] + 1)
            if kind == "qk":
                return (raw_ready, n + 1) if entry[2] < 2 else (v_ready, NH * (entry[1] + 1))
            if kind == "mt":
                return mt_ready, n + 1
            if kind == "up":
                return a_ready, n + 1
            return gated_ready, ngated(entry) + 1

        def nmasked(b, u):
            return b * sum(MASKED) + sum(MASKED[:u + 1])

        block = ctx.enter_context(nc.Block())

        @block.sync
        def _(sp):
            sp.dma_start(c_sb[:], c_t).then_inc(got["c"], 16)
            sp.dma_start(x_sb[:, 0], x[0]).then_inc(got_x[0], 16)
            sp.dma_start(wmod_sb[:, 0:2], wmod[:, 0:2]).then_inc(got_mod[0], 16)
            sp.dma_start(ident_sb[:], ident).then_inc(got["ident"], 16)
            sp.dma_start(wq_sb[:], wq).then_inc(got["wq"], 16)
            sp.dma_start(wk_sb[:], wk).then_inc(got["wk"], 16)
            sp.dma_start(wv_sb[:], wv).then_inc(got["wv"], 16)
            sp.dma_start(rope_sb[:], rope).then_inc(got["rope"], 16)
            sp.dma_start(half_sb[:], half_cols).then_inc(got["half"], 16)
            sp.dma_start(ident16_sb[:], ident16).then_inc(got["bf"], 16)
            sp.dma_start(mask16_sb[:], mask16).then_inc(got["bf"], 16)
            sp.dma_start(sel16_sb[:], sel16).then_inc(got["bf"], 16)
            sp.dma_start(x_sb[:, 1], x[1]).then_inc(got_x[1], 16)
            sp.dma_start(wmod_sb[:, 2:4], wmod[:, 2:4]).then_inc(got_mod[1], 16)
            sp.dma_start(wmod_sb[:, 4:6], wmod[:, 4:6]).then_inc(got_mod[2], 16)
            sp.dma_start(x_sb[:, 2], x[2]).then_inc(got_x[2], 16)
            sp.dma_start(x_sb[:, 3], x[3]).then_inc(got_x[3], 16)
            sp.dma_start(wo_sb[:], wo).then_inc(got["wo"], 16)
            sp.dma_start(b3_sb[:], b3.partition_broadcast(P)).then_inc(got["b3"], 16)
            sp.dma_start(b12_sb[:], b12).then_inc(got["b12"], 16)
            sp.wait_ge(mod_row, 1)
            sp.dma_start(w12_sb, w12).then_inc(got["w12"], 16)
            sp.wait_ge(mod_row, 2)
            sp.dma_start(w3_sb, w3).then_inc(got["w3"], 16)
            sp.wait_ge(gate_step, 4)
            for s in range(2):
                sp.dma_start(gate_dram[s], g_rows[32 * s:32 * s + B, :]).then_inc(gate_stored, 16)
            sp.wait_ge(gate_stored, 32)
            sp.dma_start(gate_sb[:].rearrange("p s b n -> p (s b n)"),
                         gate_dram.rearrange("s b n -> (s b n)").partition_broadcast(P)).then_inc(got_gate, 16)
            for e in SCHEDULE:
                if e[0] == "down":
                    _, b, t = e
                    n = NTH[e]
                    sp.wait_ge(out_ready, n + 1)
                    sp.dma_start(out[b, t], x_sb[:, b, t]).then_inc(stored, 16)
            sp.wait_ge(stored, 16 * B * NT)

        @block.gpsimd
        def _(pool):
            nc.gpsimd.memset(c_silu[:], 0.0).then_inc(zeroed, 1)
            nc.gpsimd.memset(eps_half[:], -0.5).then_inc(zeroed, 1)
            nc.gpsimd.memset(v_pad[:], 0.0).then_inc(zeroed, 1)
            nc.gpsimd.memset(m3[:], 0.0).then_inc(zeroed, 1)
            nc.gpsimd.memset(ones_pad[:], 0.0).then_inc(zeroed, 1)
            pool.wait_ge(zeroed, 5)
            for h in range(NH):
                nc.gpsimd.memset(ones_pad[:, h, 16 * h:16 * h + 16], 1.0).then_inc(zeroed, 1)

            for e in SCHEDULE:
                if e == ("mods", 2, 0):
                    pool.wait_ge(got_gate, 16)
                    pool.wait_ge(got["b3"], 16)
                    pool.wait_ge(mod_row, 2)
                    for b in range(B):
                        nc.gpsimd.tensor_tensor(gb3_sb[:, b], gate_sb[:, 1, b], b3_sb[:], ALU.mult).then_inc(gb3_ready, 1)
                elif e[0] == "ln":
                    _, which, b = e
                    n = NTH[e]
                    pool.wait_ge(mv_ready, NT * (n + 1))
                    if n:
                        pool.wait_ge(xn_ready, NT * n)
                    nc.gpsimd.tensor_scalar(rstd[:].unsqueeze(2), mv[:, n % 2, :, 1:2], EPS, None, ALU.add).then_inc(rstd_step, 1)
                    pool.wait_ge(rstd_step, 2 * n + 1)
                    nc.gpsimd.tensor_tensor(rstd[:], rstd[:], eps_half[:], ALU.pow).then_inc(rstd_step, 1)
                    pool.wait_ge(rstd_step, 2 * n + 2)
                    if n >= 2:
                        w0, b0 = next(f[1:] for f in SCHEDULE if f[0] == "ln" and NTH[f] == n - 2)
                        pool.wait_ge(h_ready[w0 - 1], KC * (b0 + 1))
                    for t in range(NT):
                        nc.gpsimd.tensor_scalar(xn[:, n % 2, t], x_sb[:, b, t], mv[:, n % 2, t, 0:1], rstd[:, t:t + 1],
                                                ALU.subtract, ALU.mult).then_inc(xn_ready, 1)
                    if which == 2:
                        pool.wait_ge(gb3_ready, b + 1)
                        pool.wait_ge(xn_ready, NT * (n + 1))
                        for t in range(NT):
                            nc.gpsimd.tensor_tensor(x_sb[:, b, t], x_sb[:, b, t], gb3_sb[:, b], ALU.add).then_inc(x2b_ready, 1)
                elif e[0] == "qk":
                    _, b, i = e
                    n = NTH[e]
                    w = 2 * S if i < 2 else S
                    pool.wait_ge(raw_ready, n + 1)
                    pool.wait_ge(got["rope"], 16)
                    if n >= 2:
                        pool.wait_ge(rot_ready, n - 1)
                    nc.gpsimd.tensor_tensor(
                        rcos[:, n % 2, 0:w].rearrange("p (g s) -> p g s", s=S),
                        raw[:, n % 2, 0:w].rearrange("p (g s) -> p g s", s=S),
                        rope_sb[:, 0:1, :].to_broadcast([P, w // S, S]), ALU.mult).then_inc(rcos_ready, 1)
                elif e[0] == "mt":
                    _, b, qt = e
                    n = NTH[e]
                    pool.wait_ge(max_done, 2 * G * b + G * (qt + 1))
                    if b >= 1:
                        pool.wait_ge(mt_ready, n - 1)
                    slot = m3[:, qt].rearrange("p g (j r) -> p g j r", r=32)
                    rest = mx[:, qt].rearrange("p g (j h) -> p g j h", h=NH)
                    for k in range(NPIECE):
                        if k:
                            nxt = mres[:, k - 1].rearrange("p g (j h) -> p g j h", h=NH)
                            nc.gpsimd.tensor_tensor(nxt, rest, slot[:, :, :, k - 1:k + 3:3], ALU.add).then_inc(piece, 1)
                            pool.wait_ge(piece, 5 * n + 2 * k)
                            rest = nxt
                        nc.gpsimd.tensor_scalar(slot[:, :, :, k:k + 4:3], rest, -1.0, None, ALU.mult).then_inc(piece, 1)
                        pool.wait_ge(piece, 5 * n + 2 * k + 1)
                elif e[0] == "st":
                    _, b, u = e
                    n = NTH[e]
                    if MASKED[u]:
                        pool.wait_ge(exp_done, 2 * (n + 1))
                        v = probs[:, n % 3].rearrange("p j (g q) -> p (j g) q", q=P)
                        nc.gpsimd.affine_select(out=v, in_=v, compare_op=ALU.is_ge, fill=0.0, base=0,
                                                pattern=[[0, NJ * G], [1, P]], channel_multiplier=-1).then_inc(mask_done, 1)
                elif e[0] == "wo":
                    _, b, qt = e
                    pool.wait_ge(gated_ready, ngated(e) + 1)
                    nc.gpsimd.tensor_tensor(x_sb[:, b, qt], gated[:, ngated(e) % 2], x_sb[:, b, qt], ALU.add).then_inc(x2_ready, 1)
                elif e[0] == "down":
                    _, b, t = e
                    n = NTH[e]
                    pool.wait_ge(gated_ready, ngated(e) + 1)
                    pool.wait_ge(x2b_ready, NT * (b + 1))
                    nc.gpsimd.tensor_tensor(x_sb[:, b, t], gated[:, ngated(e) % 2], x_sb[:, b, t], ALU.add).then_inc(out_ready, 1)

        @block.scalar
        def _(act):
            act.wait_ge(got["c"], 16)
            nc.scalar.activation(c_exp[:], c_sb[:], ACT.Exp, scale=-1.0).then_inc(silu_exp, 1)
            for e in SCHEDULE:
                if e[0] in GEN_KINDS:
                    bank, full, n2 = gen(e)
                if e[0] == "mods" and e[1] < 2:
                    act.wait_ge(full, n2 + 1)
                    nc.scalar.copy(modrow[:, e[1]], bank[0:64, :]).then_inc(mod_row, 1)
                elif e[0] == "qk":
                    _, b, i = e
                    n = NTH[e]
                    act.wait_ge(full, n2 + 1)
                    if n >= 2:
                        act.wait_ge(shuf_ready, n - 1)
                        act.wait_ge(rcos_ready, n - 1)
                    if i < 2:
                        nc.scalar.copy(raw[:, n % 2], bank[:]).then_inc(raw_ready, 1)
                    else:
                        nc.scalar.copy(raw[:, n % 2, 0:S], bank[:, 0:S]).then_inc(raw_ready, 1)
                        if b >= 2:
                            act.wait_ge(pv_done, NU * (b - 1))
                        act.wait_ge(zeroed, 3)
                        for h in range(NH):
                            src = bank[:, S:2 * S].rearrange("p (t h j d) -> p t h j d", t=NT, h=NH, j=NJ)
                            nc.scalar.copy(v_pad[:, b % 2, :, h, :, 16 * h:16 * h + 16], src[:, :, h]).then_inc(v_ready, 1)
                elif e[0] == "mt":
                    _, b, qt = e
                    act.wait_ge(full, n2 + 1)
                    if b >= 1:
                        act.wait_ge(st_full, NU * (b - 1) + (2 if qt == 0 else NU))
                    nc.scalar.copy(m_t[:, qt], bank[:].bitcast(BF16)[:, 0:G * P]).then_inc(mt_ready, 1)
                elif e[0] == "st":
                    n = NTH[e]
                    act.wait_ge(st_full, n + 1)
                    if n >= 3:
                        act.wait_ge(pv_done, n - 2)
                    for j in range(0, NJ, 2):
                        nc.scalar.activation(probs[:, n % 3, j:j + 2], sc_ps[:, j:j + 2], ACT.Exp,
                                             scale=DH ** -0.5).then_inc(exp_done, 1)
                elif e[0] == "up":
                    _, b, mc = e
                    n = NTH[e]
                    act.wait_ge(full, n2 + 1)
                    act.wait_ge(got["b12"], 16)
                    if n >= 2:
                        act.wait_ge(a_ready, n - 1)
                    nc.scalar.activation(act_s[:, n % 2], bank[:, 0:S], ACT.Silu, bias=b12_sb[:, mc:mc + 1]).then_inc(act_ready, 1)

        @block.vector
        def _(dve):
            dve.wait_ge(silu_exp, 1)
            dve.wait_ge(zeroed, 1)
            nc.vector.tensor_scalar(c_exp[:], c_exp[:], 1.0, None, ALU.add).then_inc(silu_step, 1)
            dve.wait_ge(silu_step, 1)
            nc.vector.reciprocal(c_exp[:], c_exp[:]).then_inc(silu_step, 1)
            dve.wait_ge(silu_step, 2)
            dve.wait_ge(got["c"], 16)
            nc.vector.tensor_tensor(c_silu[:, :, 0:B], c_sb[:], c_exp[:], ALU.mult).then_inc(silu_step, 1)

            for e in SCHEDULE:
                if e[0] in GEN_KINDS:
                    bank, full, n2 = gen(e)
                if e[0] == "modt":
                    i = e[1]
                    dve.wait_ge(full, n2 + 1)
                    v = bank[:, 0:KC * 64].rearrange("p (c r) -> p c r", r=64)
                    nc.vector.tensor_copy(shift_sb[:, i], v[:, :, 0:B]).then_inc(mod_ready, 1)
                    nc.vector.tensor_scalar(scale_sb[:, i], v[:, :, 32:32 + B], 1.0, None, ALU.add).then_inc(mod_ready, 1)
                elif e == ("mods", 2, 0):
                    dve.wait_ge(full, n2 + 1)
                    nc.vector.tensor_scalar(g_sign[:], bank[0:64, :], 0.0, 2.0, ALU.is_ge, ALU.mult).then_inc(gate_step, 1)
                    nc.vector.tensor_scalar(g_rows[:], bank[0:64, :], -1.0, GATE_MIN, ALU.mult, ALU.max).then_inc(gate_step, 1)
                    dve.wait_ge(gate_step, 2)
                    nc.vector.tensor_tensor(g_rows[:], bank[0:64, :], g_rows[:], ALU.max).then_inc(gate_step, 1)
                    dve.wait_ge(gate_step, 3)
                    nc.vector.scalar_tensor_tensor(g_rows[:], g_sign[:], -1.0, g_rows[:], ALU.add, ALU.mult).then_inc(gate_step, 1)
                elif e[0] == "ln":
                    _, which, b = e
                    n = NTH[e]
                    if which == 1:
                        dve.wait_ge(got_x[b], 16)
                    else:
                        dve.wait_ge(x2_ready, NT * (b + 1))
                    if n:
                        dve.wait_ge(mv_ready, NT * n)
                    for t in range(NT):
                        nc.vector.bn_stats(st6[:, t], x_sb[:, b, t]).then_inc(bn_done, 1)
                    dve.wait_ge(bn_done, NT * (n + 1))
                    if n >= 2:
                        dve.wait_ge(xn_ready, NT * (n - 1))
                    for t in range(NT):
                        nc.vector.bn_aggr(mv[:, n % 2, t], st6[:, t]).then_inc(mv_ready, 1)
                elif e[0] == "tr":
                    _, which, b, pair = e
                    dve.wait_ge(full, n2 + 1)
                    dve.wait_ge(mod_ready, 2 * which)
                    if which == 1 and b >= 1:
                        dve.wait_ge(v_ready, 2 * b)
                    if which == 2 and b >= 1:
                        dve.wait_ge(a_ready, MC * b)
                    for k in range(2):
                        c = 2 * pair + k
                        ins = nc.vector.tensor_scalar(h_t[which - 1][:, c], bank[:, k * S:(k + 1) * S],
                                                      scale_sb[:, which - 1, c, b:b + 1], shift_sb[:, which - 1, c, b:b + 1],
                                                      ALU.mult, ALU.add)
                        ins.then_inc(h_ready[which - 1], 1)
                elif e[0] == "qk":
                    _, b, i = e
                    n = NTH[e]
                    w = 2 * S if i < 2 else S
                    dve.wait_ge(raw_ready, n + 1)
                    dve.wait_ge(got["rope"], 16)
                    if n >= 2:
                        dve.wait_ge(rot_ready, n - 1)
                    nc.vector.stream_shuffle(shuf[:, n % 2, 0:w], raw[:, n % 2, 0:w],
                                             [16 * (r // 16) + (r % 16 + 8) % 16 for r in range(32)]).then_inc(shuf_ready, 1)
                    dve.wait_ge(shuf_ready, n + 1)
                    v = shuf[:, n % 2, 0:w].rearrange("p (g s) -> p g s", s=S)
                    nc.vector.tensor_tensor(v, v, rope_sb[:, 1:2, :].to_broadcast([P, w // S, S]), ALU.mult).then_inc(rsin_ready, 1)
                    dve.wait_ge(rsin_ready, n + 1)
                    dve.wait_ge(rcos_ready, n + 1)
                    if b >= 2:
                        dve.wait_ge(st_full, NU * (b - 1))
                    if i < 2:
                        nc.vector.tensor_tensor(q_rot[:, b % 2, 2 * i:2 * i + 2], v, rcos[:, n % 2].rearrange("p (g s) -> p g s", s=S),
                                                ALU.add).then_inc(rot_ready, 1)
                    else:
                        if b:
                            dve.wait_ge(qk_ready, NH * b)
                        nc.vector.tensor_tensor(krot[:], shuf[:, n % 2, 0:S], rcos[:, n % 2, 0:S], ALU.add).then_inc(rot_ready, 1)
                        dve.wait_ge(rot_ready, n + 1)
                        dve.wait_ge(got["half"], 16)
                        for h in range(NH):
                            nc.vector.tensor_scalar(k_pad[:, b % 2, h], krot[:], half_sb[:, h:h + 1], None, ALU.mult).then_inc(qk_ready, 1)
                elif e[0] == "max":
                    _, b, s = e
                    n = NTH[e]
                    qt, g = divmod(s, G)
                    kw = (qt + 1) * P
                    dve.wait_ge(max_full, n + 1)
                    if b >= 1 and g == 0:
                        dve.wait_ge(piece, 5 * (NT * (b - 1) + qt + 1))
                    nc.vector.reduce_max(mx[:, qt, g].rearrange("p (j h) -> p j h", h=NH),
                                         sc_ps[:, :, 0:2 * kw].rearrange("p j (h k) -> p j h k", h=NH), AX.X).then_inc(max_done, 1)
                elif e[0] == "norm":
                    _, b, qt = e
                    n = NTH[e]
                    dve.wait_ge(pv_done, NU * b + (2 if qt == 0 else NU))
                    if n:
                        dve.wait_ge(o_ready, n)
                    nc.vector.reciprocal(rsum[:], sum_ps[:]).then_inc(rsum_ready, 1)
                    dve.wait_ge(rsum_ready, n + 1)
                    if n >= 2:
                        dve.wait_ge(gated_ready, ngated(("wo", *divmod(n - 2, NT))) + 1)
                    nc.vector.tensor_tensor(o_sb[:, n % 2], ot_ps[:], rsum[:], ALU.mult).then_inc(o_ready, 1)
                elif e[0] in ("wo", "down"):
                    _, b, t = e
                    n = ngated(e)
                    branch = 0 if e[0] == "wo" else 1
                    dve.wait_ge(full, n2 + 1)
                    dve.wait_ge(got_gate, 16)
                    if n >= 2:
                        dve.wait_ge(x2_ready, sum(1 for f in SCHEDULE if f[0] == "wo" and ngated(f) <= n - 2))
                        k = sum(1 for f in SCHEDULE if f[0] == "down" and ngated(f) <= n - 2)
                        if k:
                            dve.wait_ge(out_ready, k)
                    nc.vector.tensor_tensor(gated[:, n % 2], bank[:], gate_sb[:, branch, b], ALU.mult).then_inc(gated_ready, 1)
                elif e[0] == "up":
                    _, b, mc = e
                    n = NTH[e]
                    dve.wait_ge(act_ready, n + 1)
                    if b >= 1:
                        dve.wait_ge(gated_ready, ngated(("down", b - 1, NT - 1)) + 1)
                    nc.vector.scalar_tensor_tensor(a_t[:, mc], bank[:, S:2 * S], b12_sb[:, MC + mc:MC + mc + 1], act_s[:, n % 2],
                                                   ALU.add, ALU.mult).then_inc(a_ready, 1)

        @block.tensor
        def _(pe):
            for e in SCHEDULE:
                if e[0] in GEN_KINDS:
                    bank, full, n2 = gen(e)
                    if n2:
                        pe.wait_ge(*read_out(GEN_ORDER[GEN[e] - 2]))
                if e[0] == "mods":
                    i = e[1]
                    pe.wait_ge(silu_step, 3)
                    pe.wait_ge(got_mod[i], 16)
                    for k in range(KC):
                        for s in range(2):
                            last = nc.tensor.matmul(bank[32 * s:32 * s + 32, :], c_silu[:, k], wmod_sb[:, 2 * i + s, k],
                                                    start=(k == 0), stop=(k == KC - 1), skip_group_check=True)
                    last.then_inc(full, 1)
                elif e[0] == "modt":
                    i = e[1]
                    pe.wait_ge(mod_row, i + 1)
                    pe.wait_ge(got["ident"], 16)
                    for c in range(KC):
                        last = nc.tensor.transpose(bank[:, c * 64:(c + 1) * 64], modrow[:, i, c * P:(c + 1) * P], ident_sb[0:64, 0:64])
                    last.then_inc(full, 1)
                elif e[0] == "tr":
                    _, which, b, pair = e
                    n = NTH[("ln", which, b)]
                    pe.wait_ge(xn_ready, NT * (n + 1))
                    for k in range(2):
                        c = 2 * pair + k
                        for t in range(NT):
                            last = nc.tensor.transpose(bank[:, k * S + t * P:k * S + (t + 1) * P],
                                                       xn[:, n % 2, t, c * P:(c + 1) * P], ident_sb[:])
                    last.then_inc(full, 1)
                elif e[0] == "qk":
                    _, b, i = e
                    pe.wait_ge(h_ready[0], KC * (b + 1))
                    h1 = h_t[0]
                    if i < 2:
                        pe.wait_ge(got["wq"], 16)
                        for g in (2 * i, 2 * i + 1):
                            for k in range(KC):
                                last = nc.tensor.matmul(bank[:, (g % 2) * S:(g % 2 + 1) * S], wq_sb[:, k, g], h1[:, k],
                                                        start=(k == 0), stop=(k == KC - 1))
                    else:
                        pe.wait_ge(got["wk"], 16)
                        pe.wait_ge(got["wv"], 16)
                        for k in range(KC):
                            nc.tensor.matmul(bank[:, 0:S], wk_sb[:, k], h1[:, k], start=(k == 0), stop=(k == KC - 1))
                        for t in range(NT):
                            for k in range(KC):
                                last = nc.tensor.matmul(bank[:, S + t * P:S + (t + 1) * P], h1[:, k, t * P:(t + 1) * P],
                                                        wv_sb[:, k], start=(k == 0), stop=(k == KC - 1))
                    last.then_inc(full, 1)
                elif e[0] == "max":
                    _, b, s = e
                    n = NTH[e]
                    qt, g = divmod(s, G)
                    kw = (qt + 1) * P
                    if n:
                        pe.wait_ge(max_done, n)
                    if s == 0:
                        pe.wait_ge(rot_ready, 3 * (b + 1))
                        pe.wait_ge(qk_ready, NH * (b + 1))
                        pe.wait_ge(got["bf"], 48)
                        if b:
                            pe.wait_ge(exp_done, 2 * NU * b)
                    for j in range(NJ):
                        r = slice(32 * j, 32 * j + 32)
                        nc.tensor.matmul(sc_ps[:, j, 0:2 * kw].rearrange("p (h k) -> p h k", h=NH),
                                         q_rot[r, b % 2, g, qt * P:(qt + 1) * P], k_pad[r, b % 2, :, 0:kw],
                                         start=True, stop=False, skip_group_check=True)
                    for j in range(NJ):
                        last = nc.tensor.matmul(sc_ps[:, j, 0:2 * kw].rearrange("p (h k) -> p h k", h=NH)[:, :, qt * P:kw],
                                                ident16_sb[:], mask16_sb[:].unsqueeze(1).to_broadcast([P, NH, P]),
                                                start=False, stop=True, skip_group_check=True)
                    last.then_inc(max_full, 1)
                elif e[0] == "mt":
                    _, b, qt = e
                    n = NTH[e]
                    pe.wait_ge(piece, 5 * (n + 1))
                    pe.wait_ge(got["bf"], 48)
                    out16 = bank[:].bitcast(BF16)
                    for g in range(G):
                        last = nc.tensor.transpose(out16[:, g * P:(g + 1) * P], m3[:, qt, g], ident16_sb[:])
                    last.then_inc(full, 1)
                elif e[0] == "st":
                    _, b, u = e
                    n = NTH[e]
                    qt, h, kt = UNITS[u]
                    if u == 0:
                        pe.wait_ge(max_done, 2 * G * (b + 1))
                    pe.wait_ge(mt_ready, NT * b + qt + 1)
                    if n:
                        pe.wait_ge(exp_done, 2 * n)
                    for j in range(NJ):
                        r = slice(32 * j, 32 * j + 32)
                        nc.tensor.matmul(sc_ps[:, j].rearrange("p (g q) -> p g q", q=P), k_pad[r, b % 2, h, kt * P:(kt + 1) * P],
                                         q_rot[r, b % 2, :, qt * P:(qt + 1) * P], start=True, stop=False, skip_group_check=True)
                    for j in range(NJ):
                        r = slice(32 * j, 32 * j + 32)
                        last = nc.tensor.matmul(sc_ps[:, j], sel16_sb[r, h], m_t[r, qt], start=False, stop=True,
                                                skip_group_check=True)
                    last.then_inc(st_full, 1)
                elif e[0] == "pv":
                    _, b, u = e
                    n = NTH[e]
                    qt, h, kt = UNITS[u]
                    pe.wait_ge(exp_done, 2 * (n + 1))
                    if MASKED[u]:
                        pe.wait_ge(mask_done, nmasked(b, u))
                    first, final = h == 0 and kt == 0, h == NH - 1 and kt == qt
                    if first:
                        pe.wait_ge(v_ready, 2 * (b + 1))
                        pe.wait_ge(zeroed, 7)
                        if NT * b + qt:
                            pe.wait_ge(o_ready, NT * b + qt)
                    for j in range(NJ):
                        r = slice(32 * j, 32 * j + 32)
                        nc.tensor.matmul(ot_ps[r, :], v_pad[:, b % 2, kt, h, j], probs[:, n % 3, j], start=first, stop=final,
                                         skip_group_check=True)
                    for j in range(NJ):
                        r = slice(32 * j, 32 * j + 32)
                        last = nc.tensor.matmul(sum_ps[r, :], ones_pad[:, h], probs[:, n % 3, j], start=first, stop=final,
                                                skip_group_check=True)
                    last.then_inc(pv_done, 1)
                elif e[0] == "wo":
                    _, b, qt = e
                    n = NTH[e]
                    pe.wait_ge(o_ready, n + 1)
                    pe.wait_ge(got["wo"], 16)
                    for g in range(G):
                        last = nc.tensor.matmul(bank[:], o_sb[:, n % 2, g * P:(g + 1) * P], wo_sb[:, g], start=(g == 0), stop=(g == G - 1))
                    last.then_inc(full, 1)
                elif e[0] == "up":
                    _, b, mc = e
                    pe.wait_ge(h_ready[1], KC * (b + 1))
                    pe.wait_ge(got["w12"], 16)
                    for s in range(2):
                        col = s * M + mc * P
                        for k in range(KC):
                            last = nc.tensor.matmul(bank[:, s * S:(s + 1) * S], w12_sb[:, k, col:col + P], h_t[1][:, k],
                                                    start=(k == 0), stop=(k == KC - 1))
                    last.then_inc(full, 1)
                elif e[0] == "down":
                    _, b, t = e
                    pe.wait_ge(a_ready, MC * (b + 1))
                    pe.wait_ge(got["w3"], 16)
                    for mc in range(MC):
                        last = nc.tensor.matmul(bank[:], a_t[:, mc, t * P:(t + 1) * P], w3_sb[:, mc], start=(mc == 0), stop=(mc == MC - 1))
                    last.then_inc(full, 1)


def constants():
    f = np.float32
    bf16 = mybir.dt.np(mybir.dt.bfloat16)
    inv_freq = f(1.0) / f(10000.0) ** (np.arange(0, DH, 2, dtype=f) / f(DH))
    freqs = np.arange(S, dtype=f)[:, None] * inv_freq[None, :]
    d = np.arange(P) % DH
    cos = np.cos(freqs)[:, d % (DH // 2)].T
    sin = np.sin(freqs)[:, d % (DH // 2)].T * np.where(d < DH // 2, f(-1), f(1))[:, None]
    rope = np.stack([cos, sin], 1).astype(f)
    row = np.arange(P)
    half_cols = np.stack([(row // DH) % 2 == h for h in range(NH)], 1).astype(f)
    ident = np.eye(P, dtype=f)
    mask16 = np.where(row[None, :] > row[:, None], f(NEG), f(0)).astype(bf16)
    sel = np.stack([(row % 32) // NPIECE == h for h in range(NH)], 1)
    sel16 = np.repeat(sel[:, :, None], P, 2).astype(bf16)
    return {"rope": rope, "half_cols": half_cols, "ident": ident, "ident16": ident.astype(bf16),
            "mask16": mask16, "sel16": sel16}


def kernel(L0_attn_x, L0_attn_Wq, L0_attn_Wk, L0_attn_Wv, L0_attn_Wo, L0_ffn_w12, L0_ffn_b12, L0_ffn_w3, L0_ffn_b3,
           L0_c, L0_wmod):
    import concourse.bacc as bacc
    from concourse.bass_utils import run_bass_kernel_spmd

    def rows(a):
        a = np.asarray(a)
        return a.reshape(a.shape[0] // P, P, *a.shape[1:]).swapaxes(0, 1)

    arrays = {
        "x": np.asarray(L0_attn_x).reshape(B, NT, P, D).transpose(0, 2, 1, 3),
        "c_t": rows(np.asarray(L0_c).T),
        "wmod": rows(np.asarray(L0_wmod).reshape(D, 6, D)[:, [0, 1, 3, 4, 2, 5]]).transpose(0, 2, 1, 3),
        "wq": rows(np.asarray(L0_attn_Wq).reshape(D, NH, NJ, G, DH).transpose(0, 3, 2, 1, 4).reshape(D, G, P)),
        "wk": rows(np.asarray(L0_attn_Wk).reshape(D, NH, NJ, DH).transpose(0, 2, 1, 3).reshape(D, P)),
        "wv": rows(np.asarray(L0_attn_Wv)),
        "wo": np.asarray(L0_attn_Wo).reshape(NH, NJ, G, DH, D).transpose(1, 0, 3, 2, 4).reshape(P, G, D),
        "w12": rows(np.asarray(L0_ffn_w12).T),
        "w3": rows(np.asarray(L0_ffn_w3).T),
        "b12": np.asarray(L0_ffn_b12).reshape(2 * MC, P).T,
        "b3": np.asarray(L0_ffn_b3).reshape(D),
        **constants(),
    }
    arrays = {k: np.ascontiguousarray(v) for k, v in arrays.items()}
    nc = bacc.Bacc("TRN2", target_bir_lowering=False, num_devices=1)
    aps = {k: nc.dram_tensor(f"in_{k}", v.shape, mybir.dt.from_np(v.dtype), kind="ExternalInput").ap() for k, v in arrays.items()}
    out = nc.dram_tensor("out", (B, NT, P, D), mybir.dt.float32, kind="ExternalOutput").ap()
    build(nc, out=out, **aps)
    r = run_bass_kernel_spmd(nc, [{f"in_{k}": v for k, v in arrays.items()}], core_ids=[0])
    return r.results[0]["out"].reshape(B, S, D)
```

```python
import numpy as np
from contextlib import ExitStack
import concourse.bass as bass
from concourse import mybir

B, S, D = 4, 256, 512
P = 128
DH = 16
NKV, G = 8, 4
KC = D // P
NT = S // P
M = 512
MC = M // P
NJ, NH = 4, 2
EPS = 1e-5
NEG = -3.0e38
GATE_MIN = 0.25
NPIECE = 3

NV = NKV
QW = G * S
PAIRS = [(0, 0), (0, 1), (1, 0), (1, 1), (0, 2), (2, 0)]
PR = DH * len(PAIRS)
SR = PR + NPIECE

MSTEPS = [(qt, part) for qt in range(NT) for part in range((qt + 1) * P * NV * G // 1024)]
NM = len(MSTEPS)
NM0 = sum(1 for qt, part in MSTEPS if qt == 0)
UNITS = [(qt, h, kt) for qt in range(NT) for h in range(NH) for kt in range(qt, -1, -1)]
NU = len(UNITS)
MASKED = [qt == kt for qt, h, kt in UNITS]


def make_schedule():
    s = [("mods", 0, 0), ("ln", 1, 0), ("xn", 1, 0), ("modt", 0, 0), ("tr", 1, 0, 0), ("tr", 1, 0, 1)]
    s += [("ln", 1, 1), ("xn", 1, 1)]
    for i in range(3):
        s += [("qk", 0, i), ("rot", 0, i), ("split", 0, i), ("low", 0, i)]
    s += [("tr", 1, 1, 0), ("tr", 1, 1, 1)]
    s += [("mods", 1, 0), ("modt", 1, 0), ("mods", 2, 0)]
    for b in range(B + 1):
        now, prev, nxt, nxt2 = b < B, b >= 1, b + 1 < B, b + 2 < B

        def at(ok, *stage):
            if ok:
                s.append(stage)

        if b == 0:
            at(True, "max", b, 0)
            at(True, "max", b, 1)
        at(nxt, "qk", b + 1, 0)
        at(now, "max", b, 2)
        at(now, "max", b, 3)
        at(now, "neg", b, 0)
        at(prev, "wo", b - 1, 1)
        at(prev, "ln", 2, b - 1)
        at(nxt, "rot", b + 1, 0)
        at(now, "max", b, 4)
        at(now, "mt", b, 0)
        at(now, "max", b, 5)
        at(nxt, "split", b + 1, 0)
        at(nxt, "qk", b + 1, 1)
        at(prev, "xn", 2, b - 1)
        at(now, "max", b, 6)
        at(nxt, "low", b + 1, 0)
        at(nxt, "rot", b + 1, 1)
        at(now, "max", b, 7)
        at(nxt, "split", b + 1, 1)
        at(prev, "tr", 2, b - 1, 0)
        at(prev, "tr", 2, b - 1, 1)
        at(nxt, "low", b + 1, 1)
        at(nxt, "qk", b + 1, 2)
        at(now, "max", b, 8)
        at(nxt, "rot", b + 1, 2)
        at(now, "max", b, 9)
        at(prev, "up", b - 1, 0)
        at(nxt, "split", b + 1, 2)
        at(now, "max", b, 10)
        at(now, "max", b, 11)
        at(now, "neg", b, 1)
        at(nxt, "low", b + 1, 2)
        at(prev, "up", b - 1, 1)
        at(now, "mt", b, 1)
        at(now, "st", b, 0)
        at(prev, "up", b - 1, 2)
        at(now, "st", b, 1)
        at(now, "pv", b, 0)
        at(prev, "up", b - 1, 3)
        at(now, "st", b, 2)
        at(now, "pv", b, 1)
        at(now, "norm", b, 0)
        at(prev, "down", b - 1, 0)
        at(now, "st", b, 3)
        at(now, "pv", b, 2)
        at(prev, "down", b - 1, 1)
        at(now, "st", b, 4)
        at(now, "wo", b, 0)
        at(now, "pv", b, 3)
        at(nxt2, "ln", 1, b + 2)
        at(now, "st", b, 5)
        at(nxt2, "xn", 1, b + 2)
        at(now, "pv", b, 4)
        at(nxt2, "tr", 1, b + 2, 0)
        at(nxt2, "tr", 1, b + 2, 1)
        at(now, "pv", b, 5)
        at(now, "norm", b, 1)
        at(nxt, "max", b + 1, 0)
        at(nxt, "max", b + 1, 1)
    return s


SCHEDULE = make_schedule()
KINDS = {e[0] for e in SCHEDULE}
NTH = {e: sum(1 for f in SCHEDULE[:n] if f[0] == e[0]) for n, e in enumerate(SCHEDULE)}
GEN_KINDS = ("mods", "modt", "tr", "qk", "mt", "wo", "up", "down")
GEN_ORDER = [e for e in SCHEDULE if e[0] in GEN_KINDS]
GEN = {e: n for n, e in enumerate(GEN_ORDER)}


def build(nc, x, c_t, wmod, wq, wk, wv, wo, w12, w3, b12, b3, rope, ident, ident16, mask16, out):
    F32, BF16 = mybir.dt.float32, mybir.dt.bfloat16
    ALU, ACT, AX = mybir.AluOpType, mybir.ActivationFunctionType, mybir.AxisListType
    ctx = ExitStack()
    with ctx:
        def sb(name, shape, dt=F32):
            return ctx.enter_context(nc.sbuf_tensor(name, shape, dt))

        def ps(name, shape, dt=F32):
            return ctx.enter_context(nc.psum_tensor(name, shape, dt))

        def sem(name):
            return ctx.enter_context(nc.semaphore(name))

        x_sb = sb("x_sb", [P, B, NT, D])
        wmod_sb = sb("wmod_sb", [P, 6, KC, D])
        wq_sb = sb("wq_sb", [P, KC, G, P])
        wk_sb = sb("wk_sb", [P, KC, P])
        wv_sb = sb("wv_sb", [P, KC, P])
        wo_sb = sb("wo_sb", [P, G, D])
        w12_sb = wmod_sb[:, 0:2].rearrange("p s k n -> p (s k n)").rearrange("p (k n) -> p k n", k=KC)
        w3_sb = wmod_sb[:, 2]
        gb3_sb = wmod_sb[:, 3]
        b12_sb = sb("b12_sb", [P, 2 * MC])
        b3_sb = sb("b3_sb", [P, D])
        rope_sb = sb("rope_sb", [P, 2, S])
        ident_sb = sb("ident_sb", [P, P])
        ident16_sb = sb("ident16_sb", [P, P], BF16)
        mask16_sb = sb("mask16_sb", [P, P], BF16)
        c_sb = sb("c_sb", [P, KC, B])
        c_exp = sb("c_exp", [P, KC, B])
        c_silu = sb("c_silu", [P, KC, 32])
        modrow = sb("modrow", [64, 2, D])
        shift_sb = sb("shift_sb", [P, 2, KC, B])
        scale_sb = sb("scale_sb", [P, 2, KC, B])
        g_sign = sb("g_sign", [64, D])
        g_rows = sb("g_rows", [64, D])
        gate_sb = sb("gate_sb", [P, 2, 2, D])
        eps_half = sb("eps_half", [P, NT])
        st6 = sb("st6", [P, NT, 6])
        mv = sb("mv", [P, 2, NT, 2])
        rstd = sb("rstd", [P, NT])
        xn = sb("xn", [P, 2, NT, D])
        h_t = [sb("h1_t", [P, KC, S]), sb("h2_t", [P, KC, S])]
        raw = sb("raw", [P, 2, 2 * S])
        shuf = sb("shuf", [P, 2, 2 * S])
        pieces = sb("pieces", [P, 2, 3, 2 * S], BF16)
        q_st0 = sb("q_st0", [P, NV * QW], BF16)
        q_st1 = wmod_sb[:, 4:6].rearrange("p s k n -> p (s k n)").bitcast(BF16)
        q_st = [q.rearrange("p (v g s) -> p v g s", v=NV, g=G) for q in (q_st0[:], q_st1)]
        k_st = sb("k_st", [P, 2, NV, S], BF16)
        v_pad = sb("v_pad", [P, 2, NT, NH, NJ, 32])
        ones_pad = sb("ones_pad", [P, NH, 32])
        mx = sb("mx", [P, NT, NV * G])
        mres = sb("mres", [P, 2, NV * G])
        m3 = sb("m3", [P, NT, NPIECE, NV * G], BF16)
        m_t = sb("m_t", [NPIECE * NV * G, NT, P], BF16)
        probs = sb("probs", [P, 3, NJ, G * P])
        rsum = sb("rsum", [P, G * P])
        o_sb = sb("o_sb", [P, 2, G * P])
        gated = sb("gated", [P, 2, D])
        act_s = sb("act_s", [P, 2, S])
        a_t = sb("a_t", [P, MC, S])

        gate_dram = nc.dram_tensor("gate_dram", (2, B, D), F32, kind="Internal").ap()

        sc_ps = ps("sc_ps", [P, NJ, 512])
        ot_ps = ps("ot_ps", [P, 512])
        sum_ps = ps("sum_ps", [P, 512])
        gen_ps = [ps("gen0_ps", [P, 512]), ps("gen1_ps", [P, 512])]

        loads = ["c", "ident", "rope", "bf", "wq", "wk", "wv", "wo", "w12", "w3", "b12", "b3"]
        got = {k: sem(f"got_{k}") for k in loads}
        got_x = [sem(f"got_x{b}") for b in range(B)]
        got_mod = [sem(f"got_mod{i}") for i in range(3)]
        gate_stored = sem("gate_stored")
        got_gate = [sem("got_gate0"), sem("got_gate1")]
        stacked_in = [[sem(f"stacked{k}_{i}") for i in range(3)] for k in range(2)]
        m_stacked = [sem("m_stacked0"), sem("m_stacked1")]
        stored = sem("stored")
        zeroed = sem("zeroed")
        silu_exp = sem("silu_exp")
        silu_step = sem("silu_step")
        gen_full = [sem("gen_full0"), sem("gen_full1")]
        mod_row = sem("mod_row")
        mod_ready = sem("mod_ready")
        gate_step = sem("gate_step")
        gb3_ready = sem("gb3_ready")
        bn_done = sem("bn_done")
        mv_ready = sem("mv_ready")
        rstd_step = sem("rstd_step")
        xn_ready = sem("xn_ready")
        h_ready = [sem("h1_ready"), sem("h2_ready")]
        raw_ready = sem("raw_ready")
        v_ready = sem("v_ready")
        rsin_ready = sem("rsin_ready")
        rcos_ready = sem("rcos_ready")
        rot_ready = sem("rot_ready")
        high_ready = sem("high_ready")
        rest_ready = sem("rest_ready")
        mid_ready = sem("mid_ready")
        low_ready = sem("low_ready")
        max_full = sem("max_full")
        max_done = sem("max_done")
        piece = sem("piece")
        mt_ready = sem("mt_ready")
        st_full = sem("st_full")
        exp_done = sem("exp_done")
        mask_done = sem("mask_done")
        pv_done = sem("pv_done")
        rsum_ready = sem("rsum_ready")
        o_ready = sem("o_ready")
        gated_ready = sem("gated_ready")
        x2_ready = sem("x2_ready")
        x2b_ready = sem("x2b_ready")
        act_ready = sem("act_ready")
        a_ready = sem("a_ready")
        out_ready = sem("out_ready")

        def gen(entry):
            n = GEN[entry]
            return gen_ps[n % 2], gen_full[n % 2], n // 2

        def ngated(entry):
            return sum(1 for f in SCHEDULE[:SCHEDULE.index(entry)] if f[0] in ("wo", "down"))

        def read_out(entry):
            kind, n = entry[0], NTH[entry]
            if kind == "mods":
                return (mod_row, entry[1] + 1) if entry[1] < 2 else (gate_step, 4)
            if kind == "modt":
                return mod_ready, 2 * (n + 1)
            if kind == "tr":
                return h_ready[entry[1] - 1], KC * entry[2] + 2 * (entry[3] + 1)
            if kind == "qk":
                return (raw_ready, n + 1) if entry[2] < 2 else (v_ready, NH * (entry[1] + 1))
            if kind == "mt":
                return mt_ready, n + 1
            if kind == "up":
                return a_ready, n + 1
            return gated_ready, ngated(entry) + 1

        def stacked(b, i):
            return stacked_in[b % 2][i], 16 * len(PAIRS) * (b // 2 + 1)

        def nmasked(b, u):
            return b * sum(MASKED) + sum(MASKED[:u + 1])

        block = ctx.enter_context(nc.Block())

        @block.sync
        def _(sp):
            sp.dma_start(c_sb[:], c_t).then_inc(got["c"], 16)
            sp.dma_start(x_sb[:, 0], x[0]).then_inc(got_x[0], 16)
            sp.dma_start(wmod_sb[:, 0:2], wmod[:, 0:2]).then_inc(got_mod[0], 16)
            sp.dma_start(ident_sb[:], ident).then_inc(got["ident"], 16)
            sp.dma_start(wq_sb[:], wq).then_inc(got["wq"], 16)
            sp.dma_start(rope_sb[:], rope).then_inc(got["rope"], 16)
            sp.dma_start(wk_sb[:], wk).then_inc(got["wk"], 16)
            sp.dma_start(wv_sb[:], wv).then_inc(got["wv"], 16)
            sp.dma_start(x_sb[:, 1], x[1]).then_inc(got_x[1], 16)
            sp.dma_start(wmod_sb[:, 2:4], wmod[:, 2:4]).then_inc(got_mod[1], 16)
            sp.dma_start(wmod_sb[:, 4:6], wmod[:, 4:6]).then_inc(got_mod[2], 16)
            sp.dma_start(ident16_sb[:], ident16).then_inc(got["bf"], 16)
            sp.dma_start(mask16_sb[:], mask16).then_inc(got["bf"], 16)

            def load_rest():
                sp.wait_ge(mod_row, 1)
                sp.dma_start(wo_sb[:], wo).then_inc(got["wo"], 16)
                sp.dma_start(b3_sb[:], b3.partition_broadcast(P)).then_inc(got["b3"], 16)
                sp.dma_start(b12_sb[:], b12).then_inc(got["b12"], 16)
                sp.dma_start(x_sb[:, 2], x[2]).then_inc(got_x[2], 16)
                sp.dma_start(w12_sb, w12).then_inc(got["w12"], 16)
                sp.wait_ge(mod_row, 2)
                sp.dma_start(w3_sb, w3).then_inc(got["w3"], 16)
                sp.dma_start(x_sb[:, 3], x[3]).then_inc(got_x[3], 16)

            def load_gates(b):
                sp.dma_start(gate_sb[:, b % 2], gate_dram[:, b].partition_broadcast(P)).then_inc(got_gate[b % 2], 16)

            for e in SCHEDULE:
                n = NTH[e]
                if e == ("mods", 2, 0):
                    sp.wait_ge(gate_step, 4)
                    for s in range(2):
                        sp.dma_start(gate_dram[s], g_rows[32 * s:32 * s + B, :]).then_inc(gate_stored, 16)
                    sp.wait_ge(gate_stored, 32)
                    load_gates(0)
                    load_gates(1)
                elif e[0] == "low":
                    _, b, i = e
                    sp.wait_ge(mid_ready, n + 1)
                    sp.wait_ge(low_ready, n + 1)
                    if b >= 2:
                        sp.wait_ge(st_full, 2 * NU * (b - 1))
                    if b == 1:
                        sp.wait_ge(gate_step, 4)
                    for slot, (pq, pk) in enumerate(PAIRS):
                        rows = slice(DH * slot, DH * slot + DH)
                        if i < 2:
                            dst, piece_n, w = q_st[b % 2][rows, :, 2 * i:2 * i + 2, :].rearrange("d v g s -> d v (g s)"), pq, 2 * S
                        else:
                            dst, piece_n, w = k_st[rows, b % 2], pk, S
                        sp.dma_start(dst, pieces[:, n % 2, piece_n, 0:w]).then_inc(stacked_in[b % 2][i], 16)
                    if n == 2:
                        load_rest()
                elif e[0] == "mt":
                    _, b, qt = e
                    sp.wait_ge(mt_ready, n + 1)
                    if b >= 2:
                        sp.wait_ge(st_full, 2 * NU * (b - 1))
                    sp.dma_start(q_st[b % 2][PR:SR, :, :, qt * P:(qt + 1) * P].rearrange("t v g s -> t (v g) s"),
                                 m_t[:, qt]).then_inc(m_stacked[qt], 16)
                elif e[0] == "down":
                    _, b, t = e
                    sp.wait_ge(out_ready, n + 1)
                    sp.dma_start(out[b, t], x_sb[:, b, t]).then_inc(stored, 16)
                    if t == NT - 1 and b + 2 < B:
                        load_gates(b + 2)
            sp.wait_ge(stored, 16 * B * NT)

        @block.gpsimd
        def _(pool):
            nc.gpsimd.memset(c_silu[:], 0.0).then_inc(zeroed, 1)
            nc.gpsimd.memset(eps_half[:], -0.5).then_inc(zeroed, 1)
            nc.gpsimd.memset(v_pad[:], 0.0).then_inc(zeroed, 1)
            pool.wait_ge(zeroed, 3)
            nc.gpsimd.memset(k_st[PR:SR], 1.0).then_inc(zeroed, 1)
            pool.wait_ge(zeroed, 4)
            nc.gpsimd.memset(ones_pad[:], 0.0).then_inc(zeroed, 1)
            pool.wait_ge(zeroed, 5)
            for h in range(NH):
                nc.gpsimd.memset(ones_pad[:, h, 16 * h:16 * h + 16], 1.0).then_inc(zeroed, 1)

            for e in SCHEDULE:
                if e[0] == "ln":
                    _, which, b = e
                    n = NTH[e]
                    pool.wait_ge(mv_ready, NT * (n + 1))
                    if n:
                        pool.wait_ge(xn_ready, NT * n)
                    nc.gpsimd.tensor_scalar(rstd[:].unsqueeze(2), mv[:, n % 2, :, 1:2], EPS, None, ALU.add).then_inc(rstd_step, 1)
                    pool.wait_ge(rstd_step, 2 * n + 1)
                    nc.gpsimd.tensor_tensor(rstd[:], rstd[:], eps_half[:], ALU.pow).then_inc(rstd_step, 1)
                    pool.wait_ge(rstd_step, 2 * n + 2)
                elif e[0] == "xn" and e[1] == 2:
                    b = e[2]
                    pool.wait_ge(got_gate[b % 2], 16 * (b // 2 + 1))
                    pool.wait_ge(got["b3"], 16)
                    pool.wait_ge(mod_row, 2)
                    nc.gpsimd.tensor_tensor(gb3_sb[:, b], gate_sb[:, b % 2, 1], b3_sb[:], ALU.mult).then_inc(gb3_ready, 1)
                    pool.wait_ge(gb3_ready, b + 1)
                    pool.wait_ge(xn_ready, NT * (NTH[e] + 1))
                    for t in range(NT):
                        nc.gpsimd.tensor_tensor(x_sb[:, b, t], x_sb[:, b, t], gb3_sb[:, b], ALU.add).then_inc(x2b_ready, 1)
                elif e[0] == "qk":
                    n = NTH[e]
                    w = 2 * S if e[2] < 2 else S
                    pool.wait_ge(rsin_ready, 2 * n + 2)
                    pool.wait_ge(got["rope"], 16)
                    v = raw[:, n % 2, 0:w].rearrange("p (g s) -> p g s", s=S)
                    nc.gpsimd.tensor_tensor(v, v, rope_sb[:, 0:1, :].to_broadcast([P, w // S, S]), ALU.mult).then_inc(rcos_ready, 1)
                elif e[0] == "low":
                    n = NTH[e]
                    w = 2 * S if e[2] < 2 else S
                    pool.wait_ge(mid_ready, n + 1)
                    nc.gpsimd.tensor_tensor(pieces[:, n % 2, 2, 0:w], shuf[:, n % 2, 0:w], pieces[:, n % 2, 1, 0:w],
                                            ALU.subtract).then_inc(low_ready, 1)
                elif e[0] == "st":
                    _, b, u = e
                    n = NTH[e]
                    if MASKED[u]:
                        pool.wait_ge(exp_done, 2 * (n + 1))
                        v = probs[:, n % 3].rearrange("p j (g q) -> p (j g) q", q=P)
                        nc.gpsimd.affine_select(out=v, in_=v, compare_op=ALU.is_ge, fill=0.0, base=0,
                                                pattern=[[0, NJ * G], [1, P]], channel_multiplier=-1).then_inc(mask_done, 1)
                elif e[0] == "wo":
                    _, b, qt = e
                    pool.wait_ge(gated_ready, ngated(e) + 1)
                    nc.gpsimd.tensor_tensor(x_sb[:, b, qt], gated[:, ngated(e) % 2], x_sb[:, b, qt], ALU.add).then_inc(x2_ready, 1)
                elif e[0] == "down":
                    _, b, t = e
                    n = NTH[e]
                    pool.wait_ge(gated_ready, ngated(e) + 1)
                    pool.wait_ge(x2b_ready, NT * (b + 1))
                    nc.gpsimd.tensor_tensor(x_sb[:, b, t], gated[:, ngated(e) % 2], x_sb[:, b, t], ALU.add).then_inc(out_ready, 1)

        @block.scalar
        def _(act):
            act.wait_ge(got["c"], 16)
            nc.scalar.activation(c_exp[:], c_sb[:], ACT.Exp, scale=-1.0).then_inc(silu_exp, 1)
            for e in SCHEDULE:
                if e[0] in GEN_KINDS:
                    bank, full, n2 = gen(e)
                if e[0] == "mods" and e[1] < 2:
                    act.wait_ge(full, n2 + 1)
                    nc.scalar.copy(modrow[:, e[1]], bank[0:64, :]).then_inc(mod_row, 1)
                elif e[0] == "qk":
                    _, b, i = e
                    n = NTH[e]
                    w = 2 * S if i < 2 else S
                    act.wait_ge(full, n2 + 1)
                    if n >= 2:
                        act.wait_ge(rest_ready, n - 1)
                    nc.scalar.copy(raw[:, n % 2, 0:w], bank[:, 0:w]).then_inc(raw_ready, 1)
                    if i == 2:
                        if b >= 2:
                            act.wait_ge(pv_done, NU * (b - 1))
                        act.wait_ge(zeroed, 3)
                        for h in range(NH):
                            src = bank[:, S:2 * S].rearrange("p (t h j d) -> p t h j d", t=NT, h=NH, j=NJ)
                            nc.scalar.copy(v_pad[:, b % 2, :, h, :, 16 * h:16 * h + 16], src[:, :, h]).then_inc(v_ready, 1)
                elif e[0] == "rot":
                    n = NTH[e]
                    w = 2 * S if e[2] < 2 else S
                    act.wait_ge(rot_ready, n + 1)
                    if n >= 2:
                        act.wait_ge(*stacked(*divmod(n - 2, 3)))
                    nc.scalar.copy(pieces[:, n % 2, 0, 0:w], raw[:, n % 2, 0:w]).then_inc(high_ready, 1)
                elif e[0] == "split":
                    n = NTH[e]
                    w = 2 * S if e[2] < 2 else S
                    act.wait_ge(rest_ready, n + 1)
                    nc.scalar.copy(pieces[:, n % 2, 1, 0:w], shuf[:, n % 2, 0:w]).then_inc(mid_ready, 1)
                elif e[0] == "mt":
                    _, b, qt = e
                    act.wait_ge(full, n2 + 1)
                    if b >= 1:
                        act.wait_ge(m_stacked[qt], 16 * b)
                    nc.scalar.copy(m_t[:, qt], bank[0:NPIECE * NV * G, :].bitcast(BF16)[:, 0:P]).then_inc(mt_ready, 1)
                elif e[0] == "st":
                    n = NTH[e]
                    if n >= 3:
                        act.wait_ge(pv_done, n - 2)
                    for j in range(0, NJ, 2):
                        act.wait_ge(st_full, 2 * n + j // 2 + 1)
                        nc.scalar.activation(probs[:, n % 3, j:j + 2], sc_ps[:, j:j + 2], ACT.Exp,
                                             scale=DH ** -0.5).then_inc(exp_done, 1)
                elif e[0] == "up":
                    _, b, mc = e
                    n = NTH[e]
                    act.wait_ge(full, n2 + 1)
                    act.wait_ge(got["b12"], 16)
                    if n >= 2:
                        act.wait_ge(a_ready, n - 1)
                    nc.scalar.activation(act_s[:, n % 2], bank[:, 0:S], ACT.Silu, bias=b12_sb[:, mc:mc + 1]).then_inc(act_ready, 1)

        @block.vector
        def _(dve):
            dve.wait_ge(silu_exp, 1)
            dve.wait_ge(zeroed, 1)
            nc.vector.tensor_scalar(c_exp[:], c_exp[:], 1.0, None, ALU.add).then_inc(silu_step, 1)
            dve.wait_ge(silu_step, 1)
            nc.vector.reciprocal(c_exp[:], c_exp[:]).then_inc(silu_step, 1)
            dve.wait_ge(silu_step, 2)
            dve.wait_ge(got["c"], 16)
            nc.vector.tensor_tensor(c_silu[:, :, 0:B], c_sb[:], c_exp[:], ALU.mult).then_inc(silu_step, 1)

            for e in SCHEDULE:
                if e[0] in GEN_KINDS:
                    bank, full, n2 = gen(e)
                if e[0] == "modt":
                    i = e[1]
                    dve.wait_ge(full, n2 + 1)
                    v = bank[:, 0:KC * 64].rearrange("p (c r) -> p c r", r=64)
                    nc.vector.tensor_copy(shift_sb[:, i], v[:, :, 0:B]).then_inc(mod_ready, 1)
                    nc.vector.tensor_scalar(scale_sb[:, i], v[:, :, 32:32 + B], 1.0, None, ALU.add).then_inc(mod_ready, 1)
                elif e == ("mods", 2, 0):
                    dve.wait_ge(full, n2 + 1)
                    nc.vector.tensor_scalar(g_sign[:], bank[0:64, :], 0.0, 2.0, ALU.is_ge, ALU.mult).then_inc(gate_step, 1)
                    nc.vector.tensor_scalar(g_rows[:], bank[0:64, :], -1.0, GATE_MIN, ALU.mult, ALU.max).then_inc(gate_step, 1)
                    dve.wait_ge(gate_step, 2)
                    nc.vector.tensor_tensor(g_rows[:], bank[0:64, :], g_rows[:], ALU.max).then_inc(gate_step, 1)
                    dve.wait_ge(gate_step, 3)
                    nc.vector.scalar_tensor_tensor(g_rows[:], g_sign[:], -1.0, g_rows[:], ALU.add, ALU.mult).then_inc(gate_step, 1)
                elif e[0] == "ln":
                    _, which, b = e
                    n = NTH[e]
                    if which == 1:
                        dve.wait_ge(got_x[b], 16)
                    else:
                        dve.wait_ge(x2_ready, NT * (b + 1))
                    if n:
                        dve.wait_ge(mv_ready, NT * n)
                    for t in range(NT):
                        nc.vector.bn_stats(st6[:, t], x_sb[:, b, t]).then_inc(bn_done, 1)
                    dve.wait_ge(bn_done, NT * (n + 1))
                    for t in range(NT):
                        nc.vector.bn_aggr(mv[:, n % 2, t], st6[:, t]).then_inc(mv_ready, 1)
                elif e[0] == "xn":
                    _, which, b = e
                    n = NTH[e]
                    dve.wait_ge(rstd_step, 2 * n + 2)
                    for t in range(NT):
                        nc.vector.tensor_scalar(xn[:, n % 2, t], x_sb[:, b, t], mv[:, n % 2, t, 0:1], rstd[:, t:t + 1],
                                                ALU.subtract, ALU.mult).then_inc(xn_ready, 1)
                elif e[0] == "tr":
                    _, which, b, pair = e
                    dve.wait_ge(full, n2 + 1)
                    dve.wait_ge(mod_ready, 2 * which)
                    if which == 1 and b >= 1:
                        dve.wait_ge(v_ready, 2 * b)
                    if which == 2 and b >= 1:
                        dve.wait_ge(a_ready, MC * b)
                    for k in range(2):
                        c = 2 * pair + k
                        ins = nc.vector.tensor_scalar(h_t[which - 1][:, c], bank[:, k * S:(k + 1) * S],
                                                      scale_sb[:, which - 1, c, b:b + 1], shift_sb[:, which - 1, c, b:b + 1],
                                                      ALU.mult, ALU.add)
                        ins.then_inc(h_ready[which - 1], 1)
                elif e[0] == "qk":
                    n = NTH[e]
                    w = 2 * S if e[2] < 2 else S
                    dve.wait_ge(raw_ready, n + 1)
                    dve.wait_ge(got["rope"], 16)
                    if n >= 2:
                        dve.wait_ge(low_ready, n - 1)
                    for lo in (0, P // 2):
                        src, dst = slice(lo, lo + P // 2), slice(P // 2 - lo, P - lo)
                        nc.vector.tensor_tensor(shuf[dst, n % 2, 0:w].rearrange("p (g s) -> p g s", s=S),
                                                raw[src, n % 2, 0:w].rearrange("p (g s) -> p g s", s=S),
                                                rope_sb[src, 1:2, :].to_broadcast([P // 2, w // S, S]), ALU.mult).then_inc(rsin_ready, 1)
                elif e[0] == "rot":
                    n = NTH[e]
                    w = 2 * S if e[2] < 2 else S
                    dve.wait_ge(rsin_ready, 2 * n + 2)
                    dve.wait_ge(rcos_ready, n + 1)
                    nc.vector.tensor_tensor(raw[:, n % 2, 0:w], raw[:, n % 2, 0:w], shuf[:, n % 2, 0:w], ALU.add).then_inc(rot_ready, 1)
                elif e[0] == "split":
                    n = NTH[e]
                    w = 2 * S if e[2] < 2 else S
                    dve.wait_ge(high_ready, n + 1)
                    dve.wait_ge(rot_ready, n + 1)
                    nc.vector.tensor_tensor(shuf[:, n % 2, 0:w], raw[:, n % 2, 0:w], pieces[:, n % 2, 0, 0:w],
                                            ALU.subtract).then_inc(rest_ready, 1)
                elif e[0] == "max":
                    _, b, s = e
                    n = NTH[e]
                    qt, part = MSTEPS[s]
                    kw = (qt + 1) * P
                    heads = 2 * 512 // kw
                    dve.wait_ge(max_full, n + 1)
                    if b >= 1 and part == 0:
                        dve.wait_ge(piece, 5 * (NT * (b - 1) + qt + 1))
                    nc.vector.reduce_max(mx[:, qt, part * heads:(part + 1) * heads],
                                         sc_ps[:, 2 * (s % 2):2 * (s % 2) + 2].rearrange("p b n -> p (b n)").rearrange("p (h k) -> p h k", k=kw),
                                         AX.X).then_inc(max_done, 1)
                elif e[0] == "neg":
                    _, b, qt = e
                    n = NTH[e]
                    dve.wait_ge(max_done, NM * b + (NM0 if qt == 0 else NM))
                    if b >= 1:
                        dve.wait_ge(mt_ready, n - 1)
                    rest = mx[:, qt]
                    for k in range(NPIECE):
                        if k:
                            nc.vector.tensor_tensor(mres[:, k - 1], rest, m3[:, qt, k - 1], ALU.add).then_inc(piece, 1)
                            dve.wait_ge(piece, 5 * n + 2 * k)
                            rest = mres[:, k - 1]
                        nc.vector.tensor_scalar(m3[:, qt, k], rest, -1.0, None, ALU.mult).then_inc(piece, 1)
                        dve.wait_ge(piece, 5 * n + 2 * k + 1)
                elif e[0] == "norm":
                    _, b, qt = e
                    n = NTH[e]
                    dve.wait_ge(pv_done, NU * b + (2 if qt == 0 else NU))
                    if n:
                        dve.wait_ge(o_ready, n)
                    nc.vector.reciprocal(rsum[:], sum_ps[:]).then_inc(rsum_ready, 1)
                    dve.wait_ge(rsum_ready, n + 1)
                    if n >= 2:
                        dve.wait_ge(gated_ready, ngated(("wo", *divmod(n - 2, NT))) + 1)
                    nc.vector.tensor_tensor(o_sb[:, n % 2], ot_ps[:], rsum[:], ALU.mult).then_inc(o_ready, 1)
                elif e[0] in ("wo", "down"):
                    _, b, t = e
                    n = ngated(e)
                    branch = 0 if e[0] == "wo" else 1
                    dve.wait_ge(full, n2 + 1)
                    dve.wait_ge(got_gate[b % 2], 16 * (b // 2 + 1))
                    if n >= 2:
                        dve.wait_ge(x2_ready, sum(1 for f in SCHEDULE if f[0] == "wo" and ngated(f) <= n - 2))
                        k = sum(1 for f in SCHEDULE if f[0] == "down" and ngated(f) <= n - 2)
                        if k:
                            dve.wait_ge(out_ready, k)
                    nc.vector.tensor_tensor(gated[:, n % 2], bank[:], gate_sb[:, b % 2, branch], ALU.mult).then_inc(gated_ready, 1)
                elif e[0] == "up":
                    _, b, mc = e
                    n = NTH[e]
                    dve.wait_ge(act_ready, n + 1)
                    if b >= 1:
                        dve.wait_ge(gated_ready, ngated(("down", b - 1, NT - 1)) + 1)
                    nc.vector.scalar_tensor_tensor(a_t[:, mc], bank[:, S:2 * S], b12_sb[:, MC + mc:MC + mc + 1], act_s[:, n % 2],
                                                   ALU.add, ALU.mult).then_inc(a_ready, 1)

        @block.tensor
        def _(pe):
            for e in SCHEDULE:
                if e[0] in GEN_KINDS:
                    bank, full, n2 = gen(e)
                    if n2:
                        pe.wait_ge(*read_out(GEN_ORDER[GEN[e] - 2]))
                if e[0] == "mods":
                    i = e[1]
                    pe.wait_ge(silu_step, 3)
                    pe.wait_ge(got_mod[i], 16)
                    for k in range(KC):
                        for s in range(2):
                            last = nc.tensor.matmul(bank[32 * s:32 * s + 32, :], c_silu[:, k], wmod_sb[:, 2 * i + s, k],
                                                    start=(k == 0), stop=(k == KC - 1), skip_group_check=True)
                    last.then_inc(full, 1)
                elif e[0] == "modt":
                    i = e[1]
                    pe.wait_ge(mod_row, i + 1)
                    pe.wait_ge(got["ident"], 16)
                    for c in range(KC):
                        last = nc.tensor.transpose(bank[:, c * 64:(c + 1) * 64], modrow[:, i, c * P:(c + 1) * P], ident_sb[0:64, 0:64])
                    last.then_inc(full, 1)
                elif e[0] == "tr":
                    _, which, b, pair = e
                    n = NTH[("xn", which, b)]
                    pe.wait_ge(xn_ready, NT * (n + 1))
                    for k in range(2):
                        c = 2 * pair + k
                        for t in range(NT):
                            last = nc.tensor.transpose(bank[:, k * S + t * P:k * S + (t + 1) * P],
                                                       xn[:, n % 2, t, c * P:(c + 1) * P], ident_sb[:])
                    last.then_inc(full, 1)
                elif e[0] == "qk":
                    _, b, i = e
                    pe.wait_ge(h_ready[0], KC * (b + 1))
                    h1 = h_t[0]
                    if i < 2:
                        pe.wait_ge(got["wq"], 16)
                        for g in (2 * i, 2 * i + 1):
                            for k in range(KC):
                                last = nc.tensor.matmul(bank[:, (g % 2) * S:(g % 2 + 1) * S], wq_sb[:, k, g], h1[:, k],
                                                        start=(k == 0), stop=(k == KC - 1))
                    else:
                        pe.wait_ge(got["wk"], 16)
                        pe.wait_ge(got["wv"], 16)
                        for k in range(KC):
                            nc.tensor.matmul(bank[:, 0:S], wk_sb[:, k], h1[:, k], start=(k == 0), stop=(k == KC - 1))
                        for t in range(NT):
                            for k in range(KC):
                                last = nc.tensor.matmul(bank[:, S + t * P:S + (t + 1) * P], h1[:, k, t * P:(t + 1) * P],
                                                        wv_sb[:, k], start=(k == 0), stop=(k == KC - 1))
                    last.then_inc(full, 1)
                elif e[0] == "max":
                    _, b, s = e
                    n = NTH[e]
                    qt, part = MSTEPS[s]
                    kw = (qt + 1) * P
                    per_bank = 512 // kw
                    if s == 0:
                        for i in range(3):
                            pe.wait_ge(*stacked(b, i))
                        pe.wait_ge(got["bf"], 32)
                    if s >= 2:
                        pe.wait_ge(max_done, n - 1)
                    elif b:
                        pe.wait_ge(exp_done, 2 * NU * b - 1 + s)
                    for k in range(2):
                        heads = sc_ps[:, 2 * (s % 2) + k].rearrange("p (h k) -> p h k", k=kw)
                        nc.tensor.matmul(heads[:, :, qt * P:kw], ident16_sb[:], mask16_sb[:].unsqueeze(1).to_broadcast([P, per_bank, P]),
                                         start=True, stop=False, skip_group_check=True)
                        for i in range(per_bank):
                            v, g = divmod((part * 2 + k) * per_bank + i, G)
                            last = nc.tensor.matmul(heads[:, i], q_st[b % 2][0:PR, v, g, qt * P:(qt + 1) * P],
                                                    k_st[0:PR, b % 2, v, 0:kw], start=False, stop=(i == per_bank - 1),
                                                    skip_group_check=True)
                    last.then_inc(max_full, 1)
                elif e[0] == "mt":
                    _, b, qt = e
                    n = NTH[e]
                    pe.wait_ge(piece, 5 * (n + 1))
                    pe.wait_ge(got["bf"], 32)
                    nc.tensor.transpose(bank[0:NPIECE * NV * G, :].bitcast(BF16)[:, 0:P],
                                        m3[:, qt].rearrange("p t h -> p (t h)"), ident16_sb[:]).then_inc(full, 1)
                elif e[0] == "st":
                    _, b, u = e
                    n = NTH[e]
                    qt, h, kt = UNITS[u]
                    if u == 0:
                        pe.wait_ge(zeroed, 4)
                    pe.wait_ge(m_stacked[qt], 16 * (b + 1))
                    for j in range(NJ):
                        if j % 2 == 0 and u == 0:
                            pe.wait_ge(max_done, NM * (b + 1) - 1 + j // 2)
                        elif j % 2 == 0:
                            pe.wait_ge(exp_done, 2 * n - 1 + j // 2)
                        v = 2 * j + h
                        last = nc.tensor.matmul(sc_ps[:, j].rearrange("p (g q) -> p g q", q=P), k_st[0:SR, b % 2, v, kt * P:(kt + 1) * P],
                                                q_st[b % 2][0:SR, v, :, qt * P:(qt + 1) * P], start=True, stop=True)
                        if j % 2 == 1:
                            last.then_inc(st_full, 1)
                elif e[0] == "pv":
                    _, b, u = e
                    n = NTH[e]
                    qt, h, kt = UNITS[u]
                    pe.wait_ge(exp_done, 2 * (n + 1))
                    if MASKED[u]:
                        pe.wait_ge(mask_done, nmasked(b, u))
                    first, final = h == 0 and kt == qt, h == NH - 1 and kt == 0
                    if first:
                        pe.wait_ge(v_ready, 2 * (b + 1))
                        pe.wait_ge(zeroed, 7)
                        if NT * b + qt:
                            pe.wait_ge(o_ready, NT * b + qt)
                    for j in range(NJ):
                        r = slice(32 * j, 32 * j + 32)
                        nc.tensor.matmul(ot_ps[r, :], v_pad[:, b % 2, kt, h, j], probs[:, n % 3, j], start=first, stop=final,
                                         skip_group_check=True)
                    for j in range(NJ):
                        r = slice(32 * j, 32 * j + 32)
                        last = nc.tensor.matmul(sum_ps[r, :], ones_pad[:, h], probs[:, n % 3, j], start=first, stop=final,
                                                skip_group_check=True)
                    last.then_inc(pv_done, 1)
                elif e[0] == "wo":
                    _, b, qt = e
                    n = NTH[e]
                    pe.wait_ge(o_ready, n + 1)
                    pe.wait_ge(got["wo"], 16)
                    for g in range(G):
                        last = nc.tensor.matmul(bank[:], o_sb[:, n % 2, g * P:(g + 1) * P], wo_sb[:, g], start=(g == 0), stop=(g == G - 1))
                    last.then_inc(full, 1)
                elif e[0] == "up":
                    _, b, mc = e
                    pe.wait_ge(h_ready[1], KC * (b + 1))
                    pe.wait_ge(got["w12"], 16)
                    for s in range(2):
                        col = s * M + mc * P
                        for k in range(KC):
                            last = nc.tensor.matmul(bank[:, s * S:(s + 1) * S], w12_sb[:, k, col:col + P], h_t[1][:, k],
                                                    start=(k == 0), stop=(k == KC - 1))
                    last.then_inc(full, 1)
                elif e[0] == "down":
                    _, b, t = e
                    pe.wait_ge(a_ready, MC * (b + 1))
                    pe.wait_ge(got["w3"], 16)
                    for mc in range(MC):
                        last = nc.tensor.matmul(bank[:], a_t[:, mc, t * P:(t + 1) * P], w3_sb[:, mc], start=(mc == 0), stop=(mc == MC - 1))
                    last.then_inc(full, 1)


def constants():
    f = np.float32
    bf16 = mybir.dt.np(mybir.dt.bfloat16)
    inv_freq = f(1.0) / f(10000.0) ** (np.arange(0, DH, 2, dtype=f) / f(DH))
    freqs = np.arange(S, dtype=f)[:, None] * inv_freq[None, :]
    d = np.arange(P) // NV
    cos = np.cos(freqs)[:, d % (DH // 2)].T
    sin = np.sin(freqs)[:, d % (DH // 2)].T * np.where(d < DH // 2, f(1), f(-1))[:, None]
    rope = np.stack([cos, sin], 1).astype(f)
    row = np.arange(P)
    ident = np.eye(P, dtype=f)
    mask16 = np.where(row[None, :] > row[:, None], f(NEG), f(0)).astype(bf16)
    return {"rope": rope, "ident": ident, "ident16": ident.astype(bf16),
            "mask16": mask16}


def kernel(L0_attn_x, L0_attn_Wq, L0_attn_Wk, L0_attn_Wv, L0_attn_Wo, L0_ffn_w12, L0_ffn_b12, L0_ffn_w3, L0_ffn_b3,
           L0_c, L0_wmod):
    import concourse.bacc as bacc
    from concourse.bass_utils import run_bass_kernel_spmd

    def rows(a):
        a = np.asarray(a)
        return a.reshape(a.shape[0] // P, P, *a.shape[1:]).swapaxes(0, 1)

    arrays = {
        "x": np.asarray(L0_attn_x).reshape(B, NT, P, D).transpose(0, 2, 1, 3),
        "c_t": rows(np.asarray(L0_c).T),
        "wmod": rows(np.asarray(L0_wmod).reshape(D, 6, D)[:, [0, 1, 3, 4, 2, 5]]).transpose(0, 2, 1, 3),
        "wq": rows(np.asarray(L0_attn_Wq).reshape(D, NH, NJ, G, DH).transpose(0, 3, 4, 2, 1).reshape(D, G, P)),
        "wk": rows(np.asarray(L0_attn_Wk).reshape(D, NH, NJ, DH).transpose(0, 3, 2, 1).reshape(D, P)),
        "wv": rows(np.asarray(L0_attn_Wv)),
        "wo": np.asarray(L0_attn_Wo).reshape(NH, NJ, G, DH, D).transpose(1, 0, 3, 2, 4).reshape(P, G, D),
        "w12": rows(np.asarray(L0_ffn_w12).T),
        "w3": rows(np.asarray(L0_ffn_w3).T),
        "b12": np.asarray(L0_ffn_b12).reshape(2 * MC, P).T,
        "b3": np.asarray(L0_ffn_b3).reshape(D),
        **constants(),
    }
    arrays = {k: np.ascontiguousarray(v) for k, v in arrays.items()}
    nc = bacc.Bacc("TRN2", target_bir_lowering=False, num_devices=1)
    aps = {k: nc.dram_tensor(f"in_{k}", v.shape, mybir.dt.from_np(v.dtype), kind="ExternalInput").ap() for k, v in arrays.items()}
    out = nc.dram_tensor("out", (B, NT, P, D), mybir.dt.float32, kind="ExternalOutput").ap()
    build(nc, out=out, **aps)
    r = run_bass_kernel_spmd(nc, [{f"in_{k}": v for k, v in arrays.items()}], core_ids=[0])
    return r.results[0]["out"].reshape(B, S, D)
```

```python
import numpy as np
from contextlib import ExitStack
import concourse.bass as bass
from concourse import mybir

B, S, D = 4, 256, 512
P = 128
DH = 16
NKV, G = 8, 4
KC = D // P
NT = S // P
M = 512
MC = M // P
NJ, NH = 4, 2
EPS = 1e-5
NEG = -3.0e38
GATE_MIN = 0.25
NPIECE = 3

NXN = 2
NV = NKV
QW = G * S
PAIRS = [(0, 0), (0, 1), (1, 0), (1, 1), (0, 2), (2, 0)]
PR = DH * len(PAIRS)
SR = PR + NPIECE

MSTEPS = [(qt, part) for qt in range(NT) for part in range((qt + 1) * P * NV * G // 1024)]
NM = len(MSTEPS)
NM0 = sum(1 for qt, part in MSTEPS if qt == 0)
UNITS = [(qt, h, kt) for qt in range(NT) for h in range(NH) for kt in range(qt, -1, -1)]
NU = len(UNITS)
MASKED = [qt == kt for qt, h, kt in UNITS]
LAST_PV = [[max(u for u in range(NU) if UNITS[u][:2] == (qt, h)) for h in range(NH)] for qt in range(NT)]
SWAP = [(p + 16) % 32 for p in range(32)]


FIRST = """
    ln.1.0.0 ln.1.0.1 mods.0.0 xn.1.0.0 xn.1.0.1 modt.0.0 tr.1.0.0 tr.1.0.1 qk.0.0 ln.1.1.0 ln.1.1.1 qk.0.1 rot.0.0
    low.0.0 rot.0.1 split.0.0 low.0.1 qk.0.2 split.0.1 rot.0.2 mods.1.0 xn.1.1.0 split.0.2 xn.1.1.1 low.0.2 tr.1.1.0
    tr.1.1.1 mods.2.0 max.0.0 max.0.1 qk.1.0 max.0.2 wsplit.0 max.0.3 neg.0.0 rot.1.0 max.0.4 qk.1.1 mt.0.0 low.1.0
    split.1.0 max.0.5 rot.1.1 max.0.6 qk.1.2 max.0.7 max.0.8 wsplit.1 max.0.9 max.0.10 max.0.11 st.0.0 neg.0.1
    ln.1.2.0 mt.0.1 low.1.1 st.0.1 ln.1.2.1 modt.1.0 split.1.1 st.0.2 xn.1.2.0 rot.1.2 keep.0.0 split.1.2 low.1.2
    xn.1.2.1 pv.0.0 pv.0.1 st.0.3 st.0.4 st.0.5 pv.0.2 norm.0.0 tr.1.2.0 tr.1.2.1 pv.0.3 max.1.0 pv.0.4 osplit.0.0
    norm.0.1 pv.0.5 keep.0.1 wo.0.0 osplit.0.1 max.1.1
"""
MIDDLE = """
    max.0.2 ln.2.-1.0 qk.1.0 max.0.3 max.0.4 wo.-1.1 rot.1.0 max.0.5 xn.2.-1.0 neg.0.0 max.0.6 qk.1.1 mt.0.0
    split.1.0 max.0.7 tr.2.-1.0 ln.2.-1.1 rot.1.1 low.1.0 ln.1.2.0 xn.2.-1.1 max.0.8 qk.1.2 max.0.9 up.-1.0.0
    split.1.1 max.0.10 max.0.11 tr.2.-1.1 xn.1.2.0 ln.1.2.1 up.-1.0.1 low.1.1 neg.0.1 st.0.0 up.-1.1.0 mt.0.1 st.0.1
    rot.1.2 pv.0.0 low.1.2 tr.1.2.0 asplit.-1.0 up.-1.1.1 keep.0.0 split.1.2 st.0.2 xn.1.2.1 down.-1.0 tr.1.2.1
    pv.0.1 st.0.3 st.0.4 norm.0.0 pv.0.2 st.0.5 asplit.-1.1 max.1.0 pv.0.3 pv.0.4 pv.0.5 osplit.0.0 keep.0.1
    norm.0.1 wo.0.0 osplit.0.1 max.1.1 down.-1.1
"""
LAST = """
    ln.2.2.0 max.3.2 wo.2.1 max.3.3 max.3.4 xn.2.2.0 max.3.5 max.3.6 tr.2.2.0 neg.3.0 max.3.7 max.3.8 ln.2.2.1
    up.2.0.0 xn.2.2.1 max.3.9 mt.3.0 max.3.10 tr.2.2.1 up.2.0.1 max.3.11 asplit.2.0 neg.3.1 st.3.0 up.2.1.0 mt.3.1
    st.3.1 pv.3.0 up.2.1.1 st.3.2 down.2.0 asplit.2.1 pv.3.1 keep.3.0 st.3.3 st.3.4 norm.3.0 pv.3.2 st.3.5 pv.3.3
    osplit.3.0 pv.3.4 pv.3.5 norm.3.1 down.2.1 keep.3.1 osplit.3.1 wo.3.0 ln.2.3.0 xn.2.3.0 wo.3.1 tr.2.3.0 ln.2.3.1
    xn.2.3.1 up.3.0.0 tr.2.3.1 up.3.0.1 up.3.1.0 asplit.3.0 up.3.1.1 asplit.3.1 down.3.0 down.3.1
"""


def make_schedule():
    def stages(text, b0):
        for word in text.split():
            kind, *numbers = word.split(".")
            numbers = [int(i) for i in numbers]
            at = 1 if kind in ("ln", "xn", "tr") else 0
            if kind not in ("mods", "modt", "wsplit"):
                numbers[at] += b0
                if numbers[at] >= B:
                    continue
            yield (kind, *numbers)

    return [*stages(FIRST, 0), *stages(MIDDLE, 1), *stages(MIDDLE, 2), *stages(LAST, 0)]


SCHEDULE = make_schedule()
KINDS = {e[0] for e in SCHEDULE}
NTH = {e: sum(1 for f in SCHEDULE[:n] if f[0] == e[0]) for n, e in enumerate(SCHEDULE)}
GEN_KINDS = ("mods", "modt", "tr", "qk", "mt", "wo", "up", "down")
GEN_ORDER = [e for e in SCHEDULE if e[0] in GEN_KINDS]
GEN = {e: n for n, e in enumerate(GEN_ORDER)}


def build(nc, x, c_t, wmod, wq, wk, wv, wo, w12, w3, b12, b3, rope, ident, ident16, mask16, halves, out):
    F32, F32R, BF16 = mybir.dt.float32, mybir.dt.float32r, mybir.dt.bfloat16
    ALU, ACT, AX = mybir.AluOpType, mybir.ActivationFunctionType, mybir.AxisListType
    ctx = ExitStack()
    with ctx:
        def sb(name, shape, dt=F32):
            return ctx.enter_context(nc.sbuf_tensor(name, shape, dt))

        def ps(name, shape, dt=F32):
            return ctx.enter_context(nc.psum_tensor(name, shape, dt))

        def sem(name):
            return ctx.enter_context(nc.semaphore(name))

        x_sb = sb("x_sb", [P, B, NT, D])
        wmod_sb = [sb("wmod0_sb", [P, 2, KC, D])]
        with nc.sbuf_tensor("wmod1_sb", [P, 2, KC, D], F32) as t:
            wmod_sb.append(t)
        w3_hi, w3_lo = sb("w3_hi", [P, MC, D], F32R), sb("w3_lo", [P, MC, D], F32R)
        wmod_sb.append(sb("wmod2_sb", [P, 2, KC, D]))
        wq_sb = sb("wq_sb", [P, KC, G, P])
        wk_sb = sb("wk_sb", [P, KC, P])
        wv_sb = sb("wv_sb", [P, KC, P])
        wo_hi, wo_lo = sb("wo_hi", [P, G, D], F32R), sb("wo_lo", [P, G, D], F32R)
        w12_sb = wmod_sb[0][:].rearrange("p s k n -> p (s k n)").rearrange("p (k n) -> p k n", k=KC)
        gb3_sb = sb("gb3_sb", [P, D])
        b12_sb = sb("b12_sb", [P, 2 * MC])
        b3_sb = sb("b3_sb", [P, D])
        rope_sb = sb("rope_sb", [P, 2, S])
        ident_sb = sb("ident_sb", [P, P])
        ident16_sb = sb("ident16_sb", [P, P], BF16)
        mask16_sb = sb("mask16_sb", [P, P], BF16)
        c_sb = sb("c_sb", [P, KC, B])
        c_exp = sb("c_exp", [P, KC, B])
        c_silu = sb("c_silu", [P, KC, 32])
        shift_sb = sb("shift_sb", [P, 2, KC, B])
        scale_sb = sb("scale_sb", [P, 2, KC, B])
        with ExitStack() as early:
            modrow = early.enter_context(nc.sbuf_tensor("modrow", [64, 2, D], F32))
            g_sign = early.enter_context(nc.sbuf_tensor("g_sign", [64, D], F32))
            g_rows = early.enter_context(nc.sbuf_tensor("g_rows", [64, D], F32))
        z_sb = sb("z_sb", [P, G * P])
        act_s = sb("act_s", [P, 2, 2, P])
        o_hi = sb("o_hi", [P, 2, G * P], F32R)
        gate_sb = sb("gate_sb", [P, 2, D])
        minus_half = sb("minus_half", [P, 1])
        st6 = sb("st6", [P, NXN, 6])
        mv = sb("mv", [P, NXN, 2])
        var_eps = sb("var_eps", [P, NXN])
        rstd = sb("rstd", [P, NXN])
        xn = sb("xn", [P, NXN, D])
        h_t = [sb("h1_t", [P, KC, S]), sb("h2_t", [P, KC, S])]
        raw = sb("raw", [P, 2, 2 * S])
        shuf = sb("shuf", [P, 2, 2 * S])
        pieces = sb("pieces", [P, 2, 3, 2 * S], BF16)
        q_st0 = sb("q_st0", [P, NV * QW], BF16)
        q_st1 = wmod_sb[2][:].rearrange("p s k n -> p (s k n)").bitcast(BF16)
        q_st = [q.rearrange("p (v g s) -> p v g s", v=NV, g=G) for q in (q_st0[:], q_st1)]
        k_st = sb("k_st", [P, 2, NV, S], BF16)
        v1 = sb("v1", [P, 2, NT, NH, NJ, 32])
        halves_sb = sb("halves_sb", [P, NH])
        mx = sb("mx", [P, NT, NV * G])
        mres = sb("mres", [P, 2, NV * G])
        m3 = sb("m3", [P, NT, NPIECE, NV * G], BF16)
        m_t = sb("m_t", [NPIECE * NV * G, NT, P], BF16)
        probs = sb("probs", [P, 3, NJ, G * P])
        with nc.sbuf_tensor("o_sb", [P, 2, G * P], F32) as o_sb:
            pass
        o_lo = sb("o_lo", [P, 2, G * P], F32R)
        gated = sb("gated", [P, 2, D])
        a_hi = sb("a_hi", [P, MC, S], F32R)
        with nc.sbuf_tensor("a_t", [P, MC, S], F32) as a_t:
            pass
        a_lo = sb("a_lo", [P, MC, S], F32R)
        raw_w = [probs[:, 1].rearrange("p j n -> p (j n)"), probs[:, 2].rearrange("p j n -> p (j n)")]

        gate_dram = nc.dram_tensor("gate_dram", (2, B, D), F32, kind="Internal").ap()

        sc_ps = ps("sc_ps", [P, NJ, 512])
        pv_ps = [ps("pv0_ps", [P, 512]), ps("pv1_ps", [P, 512])]
        gen_ps = [ps("gen0_ps", [P, 512]), ps("gen1_ps", [P, 512])]

        loads = ["c", "halves", "ident", "rope", "bf", "wq", "wk", "wv", "wo", "w12", "w3", "b12", "b3"]
        got = {k: sem(f"got_{k}") for k in loads}
        got_x = [sem(f"got_x{b}") for b in range(B)]
        got_mod = [[sem(f"got_mod{i}_{k}") for k in range(KC)] for i in range(3)]
        gate_stored = sem("gate_stored")
        got_gate = [sem("got_gate0"), sem("got_gate1")]
        stacked_in = [[sem(f"stacked{k}_{i}") for i in range(3)] for k in range(2)]
        m_stacked = [sem("m_stacked0"), sem("m_stacked1")]
        stored = sem("stored")
        zeroed = sem("zeroed")
        silu_exp = sem("silu_exp")
        silu_step = sem("silu_step")
        gen_full = [sem("gen_full0"), sem("gen_full1")]
        mod_row = sem("mod_row")
        mod_ready = sem("mod_ready")
        gate_step = sem("gate_step")
        gb3_ready = sem("gb3_ready")
        bn_done = sem("bn_done")
        mv_ready = sem("mv_ready")
        veps_ready = sem("veps_ready")
        rstd_ready = sem("rstd_ready")
        xn_ready = sem("xn_ready")
        h_ready = [sem("h1_ready"), sem("h2_ready")]
        raw_ready = sem("raw_ready")
        v_ready = sem("v_ready")
        rsin_ready = sem("rsin_ready")
        rcos_ready = sem("rcos_ready")
        rot_ready = sem("rot_ready")
        high_ready = sem("high_ready")
        rest_ready = sem("rest_ready")
        mid_ready = sem("mid_ready")
        low_ready = sem("low_ready")
        max_full = sem("max_full")
        max_done = sem("max_done")
        piece = sem("piece")
        mt_ready = sem("mt_ready")
        st_full = sem("st_full")
        exp_done = sem("exp_done")
        mask_done = sem("mask_done")
        pv_done = sem("pv_done")
        kept = sem("kept")
        w_hi = sem("w_hi")
        w_lo = sem("w_lo")
        o_hi_ready = sem("o_hi_ready")
        o_lo_ready = sem("o_lo_ready")
        a_hi_ready = sem("a_hi_ready")
        a_lo_ready = sem("a_lo_ready")
        norm_step = sem("norm_step")
        o_ready = sem("o_ready")
        gated_ready = sem("gated_ready")
        x2_ready = sem("x2_ready")
        x2b_ready = sem("x2b_ready")
        act_ready = sem("act_ready")
        a_ready = sem("a_ready")
        out_ready = sem("out_ready")

        def gen(entry):
            n = GEN[entry]
            return gen_ps[n % 2], gen_full[n % 2], n // 2

        def ngated(entry):
            return sum(1 for f in SCHEDULE[:SCHEDULE.index(entry)] if f[0] in ("wo", "down"))

        def read_out(entry):
            kind, n = entry[0], NTH[entry]
            if kind == "mods":
                return (mod_row, entry[1] + 1) if entry[1] < 2 else (gate_step, 4)
            if kind == "modt":
                return mod_ready, 2 * (n + 1)
            if kind == "tr":
                return h_ready[entry[1] - 1], NT * entry[2] + entry[3] + 1
            if kind == "qk":
                return (raw_ready, n + 1) if entry[2] < 2 else (v_ready, NH * (entry[1] + 1))
            if kind == "mt":
                return mt_ready, n + 1
            if kind == "up":
                return a_ready, n + 1
            return gated_ready, ngated(entry) + 1

        def stacked(b, i):
            return stacked_in[b % 2][i], 16 * len(PAIRS) * (b // 2 + 1)

        def nmasked(b, u):
            return b * sum(MASKED) + sum(MASKED[:u + 1])

        block = ctx.enter_context(nc.Block())

        @block.sync
        def _(sp):
            def load_mod(i):
                for k in range(KC):
                    sp.dma_start(wmod_sb[i][:, :, k], wmod[:, 2 * i:2 * i + 2, k]).then_inc(got_mod[i][k], 16)

            sp.dma_start(c_sb[:], c_t).then_inc(got["c"], 16)
            sp.dma_start(x_sb[:, 0], x[0]).then_inc(got_x[0], 16)
            load_mod(0)
            sp.dma_start(ident_sb[:], ident).then_inc(got["ident"], 16)
            sp.dma_start(wq_sb[:], wq).then_inc(got["wq"], 16)
            sp.dma_start(rope_sb[:], rope).then_inc(got["rope"], 16)
            sp.dma_start(wk_sb[:], wk).then_inc(got["wk"], 16)
            sp.dma_start(wv_sb[:], wv).then_inc(got["wv"], 16)
            sp.dma_start(x_sb[:, 1], x[1]).then_inc(got_x[1], 16)
            load_mod(1)
            load_mod(2)
            sp.dma_start(halves_sb[:], halves).then_inc(got["halves"], 16)
            sp.dma_start(ident16_sb[:], ident16).then_inc(got["bf"], 16)
            sp.dma_start(mask16_sb[:], mask16).then_inc(got["bf"], 16)

            def load_rest():
                sp.dma_start(raw_w[0], wo.rearrange("p g n -> p (g n)")).then_inc(got["wo"], 16)
                sp.dma_start(raw_w[1], w3.rearrange("p g n -> p (g n)")).then_inc(got["w3"], 16)
                sp.dma_start(b3_sb[:], b3.partition_broadcast(P)).then_inc(got["b3"], 16)
                sp.dma_start(b12_sb[:], b12).then_inc(got["b12"], 16)
                sp.dma_start(x_sb[:, 2], x[2]).then_inc(got_x[2], 16)
                sp.wait_ge(mod_row, 1)
                sp.dma_start(w12_sb, w12).then_inc(got["w12"], 16)
                sp.dma_start(x_sb[:, 3], x[3]).then_inc(got_x[3], 16)

            def load_gate(branch, b):
                sp.dma_start(gate_sb[:, branch], gate_dram[branch, b].partition_broadcast(P)).then_inc(got_gate[branch], 16)

            for e in SCHEDULE:
                n = NTH[e]
                if e == ("mods", 2, 0):
                    sp.wait_ge(gate_step, 4)
                    for s in range(2):
                        sp.dma_start(gate_dram[s], g_rows[32 * s:32 * s + B, :]).then_inc(gate_stored, 16)
                    sp.wait_ge(gate_stored, 32)
                    load_gate(0, 0)
                    load_gate(1, 0)
                elif e[0] == "low":
                    _, b, i = e
                    sp.wait_ge(mid_ready, n + 1)
                    sp.wait_ge(low_ready, n + 1)
                    if b >= 2:
                        sp.wait_ge(st_full, 2 * NU * (b - 1))
                    if b == 1:
                        sp.wait_ge(gate_step, 4)
                    for slot, (pq, pk) in enumerate(PAIRS):
                        rows = slice(DH * slot, DH * slot + DH)
                        if i < 2:
                            dst, piece_n, w = q_st[b % 2][rows, :, 2 * i:2 * i + 2, :].rearrange("d v g s -> d v (g s)"), pq, 2 * S
                        else:
                            dst, piece_n, w = k_st[rows, b % 2], pk, S
                        sp.dma_start(dst, pieces[:, n % 2, piece_n, 0:w]).then_inc(stacked_in[b % 2][i], 16)
                    if n == 2:
                        load_rest()
                elif e[0] == "mt":
                    _, b, qt = e
                    sp.wait_ge(mt_ready, n + 1)
                    if b >= 2:
                        sp.wait_ge(st_full, 2 * NU * (b - 1))
                    sp.dma_start(q_st[b % 2][PR:SR, :, :, qt * P:(qt + 1) * P].rearrange("t v g s -> t (v g) s"),
                                 m_t[:, qt]).then_inc(m_stacked[qt], 16)
                elif e[0] == "down":
                    _, b, t = e
                    sp.wait_ge(out_ready, n + 1)
                    sp.dma_start(out[b, t], x_sb[:, b, t]).then_inc(stored, 16)
                    if t == NT - 1 and b + 1 < B:
                        sp.wait_ge(gated_ready, ngated(e) + 1)
                        load_gate(1, b + 1)
                elif e[0] == "xn" and e[1] == 2 and e[3] == 0 and e[2] + 1 < B:
                    b = e[2]
                    sp.wait_ge(gated_ready, ngated(("wo", b, NT - 1)) + 1)
                    load_gate(0, b + 1)
            sp.wait_ge(stored, 16 * B * NT)

        @block.gpsimd
        def _(pool):
            nc.gpsimd.memset(c_silu[:], 0.0).then_inc(zeroed, 1)
            nc.gpsimd.memset(minus_half[:], -0.5).then_inc(zeroed, 1)
            nc.gpsimd.memset(v1[:], 1.0).then_inc(zeroed, 1)
            pool.wait_ge(zeroed, 3)
            nc.gpsimd.memset(k_st[PR:SR], 1.0).then_inc(zeroed, 1)

            for e in SCHEDULE:
                if e[0] == "ln":
                    n = NTH[e]
                    pool.wait_ge(veps_ready, n + 1)
                    pool.wait_ge(zeroed, 4)
                    nc.gpsimd.tensor_tensor(rstd[:, n % NXN:n % NXN + 1], var_eps[:, n % NXN:n % NXN + 1], minus_half[:],
                                            ALU.pow).then_inc(rstd_ready, 1)
                elif e[0] == "asplit":
                    _, b, t = e
                    if t == 0:
                        pool.wait_ge(got_gate[1], 16 * (b + 1))
                        pool.wait_ge(got["b3"], 16)
                        if b:
                            pool.wait_ge(x2b_ready, NT * b)
                        nc.gpsimd.tensor_tensor(gb3_sb[:], gate_sb[:, 1], b3_sb[:], ALU.mult).then_inc(gb3_ready, 1)
                        pool.wait_ge(gb3_ready, b + 1)
                    pool.wait_ge(xn_ready, NTH[("xn", 2, b, t)] + 1)
                    nc.gpsimd.tensor_tensor(x_sb[:, b, t], x_sb[:, b, t], gb3_sb[:], ALU.add).then_inc(x2b_ready, 1)
                elif e[0] == "qk":
                    n = NTH[e]
                    w = 2 * S if e[2] < 2 else S
                    pool.wait_ge(rsin_ready, 2 * n + 2)
                    pool.wait_ge(got["rope"], 16)
                    v = raw[:, n % 2, 0:w].rearrange("p (g s) -> p g s", s=S)
                    nc.gpsimd.tensor_tensor(v, v, rope_sb[:, 0:1, :].to_broadcast([P, w // S, S]), ALU.mult).then_inc(rcos_ready, 1)
                elif e[0] == "low":
                    n = NTH[e]
                    w = 2 * S if e[2] < 2 else S
                    pool.wait_ge(mid_ready, n + 1)
                    nc.gpsimd.tensor_tensor(pieces[:, n % 2, 2, 0:w], shuf[:, n % 2, 0:w], pieces[:, n % 2, 1, 0:w],
                                            ALU.subtract).then_inc(low_ready, 1)
                elif e[0] == "st":
                    _, b, u = e
                    n = NTH[e]
                    if MASKED[u]:
                        pool.wait_ge(exp_done, 2 * (n + 1))
                        v = probs[:, n % 3].rearrange("p j (g q) -> p (j g) q", q=P)
                        nc.gpsimd.affine_select(out=v, in_=v, compare_op=ALU.is_ge, fill=0.0, base=0,
                                                pattern=[[0, NJ * G], [1, P]], channel_multiplier=-1).then_inc(mask_done, 1)
                elif e[0] == "wo":
                    _, b, qt = e
                    pool.wait_ge(gated_ready, ngated(e) + 1)
                    nc.gpsimd.tensor_tensor(x_sb[:, b, qt], gated[:, ngated(e) % 2], x_sb[:, b, qt], ALU.add).then_inc(x2_ready, 1)
                elif e[0] == "wsplit":
                    pool.wait_ge(w_hi, e[1] + 1)
                    hi, lo = ((wo_hi, wo_lo), (w3_hi, w3_lo))[e[1]]
                    nc.gpsimd.tensor_tensor(lo[:].rearrange("p k n -> p (k n)"), raw_w[e[1]], hi[:].rearrange("p k n -> p (k n)").bitcast(F32),
                                            ALU.subtract).then_inc(w_lo, 1)
                elif e[0] == "down":
                    _, b, t = e
                    n = NTH[e]
                    pool.wait_ge(gated_ready, ngated(e) + 1)
                    pool.wait_ge(x2b_ready, NT * b + t + 1)
                    nc.gpsimd.tensor_tensor(x_sb[:, b, t], gated[:, ngated(e) % 2], x_sb[:, b, t], ALU.add).then_inc(out_ready, 1)

        @block.scalar
        def _(act):
            act.wait_ge(got["c"], 16)
            nc.scalar.activation(c_exp[:], c_sb[:], ACT.Exp, scale=-1.0).then_inc(silu_exp, 1)
            for e in SCHEDULE:
                if e[0] in GEN_KINDS:
                    bank, full, n2 = gen(e)
                if e[0] == "mods" and e[1] < 2:
                    act.wait_ge(full, n2 + 1)
                    nc.scalar.copy(modrow[:, e[1]], bank[0:64, :]).then_inc(mod_row, 1)
                elif e[0] == "qk":
                    _, b, i = e
                    n = NTH[e]
                    w = 2 * S if i < 2 else S
                    act.wait_ge(full, n2 + 1)
                    if n >= 2:
                        act.wait_ge(rest_ready, n - 1)
                    nc.scalar.copy(raw[:, n % 2, 0:w], bank[:, 0:w]).then_inc(raw_ready, 1)
                    if i == 2:
                        if b >= 2:
                            act.wait_ge(pv_done, NU * (b - 1))
                        act.wait_ge(zeroed, 3)
                        for h in range(NH):
                            src = bank[:, S:2 * S].rearrange("p (t h j d) -> p t h j d", t=NT, h=NH, j=NJ)
                            nc.scalar.copy(v1[:, b % 2, :, h, :, 16 * h:16 * h + 16], src[:, :, h]).then_inc(v_ready, 1)
                elif e[0] == "rot":
                    n = NTH[e]
                    w = 2 * S if e[2] < 2 else S
                    act.wait_ge(rot_ready, n + 1)
                    if n >= 2:
                        act.wait_ge(*stacked(*divmod(n - 2, 3)))
                    nc.scalar.copy(pieces[:, n % 2, 0, 0:w], raw[:, n % 2, 0:w]).then_inc(high_ready, 1)
                elif e[0] == "split":
                    n = NTH[e]
                    w = 2 * S if e[2] < 2 else S
                    act.wait_ge(rest_ready, n + 1)
                    nc.scalar.copy(pieces[:, n % 2, 1, 0:w], shuf[:, n % 2, 0:w]).then_inc(mid_ready, 1)
                elif e[0] == "mt":
                    _, b, qt = e
                    act.wait_ge(full, n2 + 1)
                    if b >= 1:
                        act.wait_ge(m_stacked[qt], 16 * b)
                    nc.scalar.copy(m_t[:, qt], bank[0:NPIECE * NV * G, :].bitcast(BF16)[:, 0:P]).then_inc(mt_ready, 1)
                elif e[0] == "st":
                    n = NTH[e]
                    if n >= 3:
                        act.wait_ge(pv_done, n - 2)
                    for j in range(0, NJ, 2):
                        act.wait_ge(st_full, 2 * n + j // 2 + 1)
                        if n in (1, 2):
                            act.wait_ge(w_lo, n)
                        nc.scalar.activation(probs[:, n % 3, j:j + 2], sc_ps[:, j:j + 2], ACT.Exp,
                                             scale=DH ** -0.5).then_inc(exp_done, 1)
                elif e[0] == "wsplit":
                    act.wait_ge(got["wo" if e[1] == 0 else "w3"], 16)
                    act.wait_ge(mod_row, 2)
                    hi = (wo_hi, w3_hi)[e[1]]
                    nc.scalar.copy(hi[:].rearrange("p k n -> p (k n)"), raw_w[e[1]]).then_inc(w_hi, 1)
                elif e[0] == "osplit":
                    n = NTH[e]
                    for c in range(2):
                        act.wait_ge(o_ready, 2 * n + 1 + c)
                        w = slice(c * 2 * P, (c + 1) * 2 * P)
                        nc.scalar.copy(o_hi[:, n % 2, w], o_sb[:, n % 2, w]).then_inc(o_hi_ready, 1)
                elif e[0] == "asplit":
                    _, b, t = e
                    act.wait_ge(a_ready, NTH[("up", b, t, 1)] + 1)
                    nc.scalar.copy(a_hi[:, :, t * P:(t + 1) * P], a_t[:, :, t * P:(t + 1) * P]).then_inc(a_hi_ready, 1)
                elif e[0] == "keep":
                    _, b, qt = e
                    n = NTH[e]
                    act.wait_ge(got["halves"], 16)
                    act.wait_ge(pv_done, NU * b + LAST_PV[qt][0] + 1)
                    if n == 0:
                        act.wait_ge(gate_stored, 32)
                    if n >= 2:
                        act.wait_ge(gated_ready, ngated(("wo", *divmod(n - 2, NT))) + 1)
                    nc.scalar.activation(o_sb[:, n % 2], pv_ps[0][:], ACT.Copy, scale=halves_sb[:, 0:1]).then_inc(kept, 1)
                    if n:
                        act.wait_ge(o_ready, 2 * n)
                    nc.scalar.activation(z_sb[:], pv_ps[0][:], ACT.Copy, scale=halves_sb[:, 1:2]).then_inc(kept, 1)
                elif e[0] == "up":
                    _, b, t, i = e
                    n = NTH[e]
                    act.wait_ge(full, n2 + 1)
                    act.wait_ge(got["b12"], 16)
                    if n >= 2:
                        act.wait_ge(a_ready, n - 1)
                    for m in range(2):
                        mc = 2 * i + m
                        ins = nc.scalar.activation(act_s[:, n % 2, m], bank[:, m * P:(m + 1) * P], ACT.Silu, bias=b12_sb[:, mc:mc + 1])
                    ins.then_inc(act_ready, 1)

        @block.vector
        def _(dve):
            dve.wait_ge(silu_exp, 1)
            dve.wait_ge(zeroed, 1)
            nc.vector.tensor_scalar(c_exp[:], c_exp[:], 1.0, None, ALU.add).then_inc(silu_step, 1)
            dve.wait_ge(silu_step, 1)
            nc.vector.reciprocal(c_exp[:], c_exp[:]).then_inc(silu_step, 1)
            dve.wait_ge(silu_step, 2)
            dve.wait_ge(got["c"], 16)
            nc.vector.tensor_tensor(c_silu[:, :, 0:B], c_sb[:], c_exp[:], ALU.mult).then_inc(silu_step, 1)

            for e in SCHEDULE:
                if e[0] in GEN_KINDS:
                    bank, full, n2 = gen(e)
                if e[0] == "modt":
                    i = e[1]
                    dve.wait_ge(full, n2 + 1)
                    v = bank[:, 0:KC * 64].rearrange("p (c r) -> p c r", r=64)
                    nc.vector.tensor_copy(shift_sb[:, i], v[:, :, 0:B]).then_inc(mod_ready, 1)
                    nc.vector.tensor_scalar(scale_sb[:, i], v[:, :, 32:32 + B], 1.0, None, ALU.add).then_inc(mod_ready, 1)
                elif e == ("mods", 2, 0):
                    dve.wait_ge(full, n2 + 1)
                    nc.vector.tensor_scalar(g_sign[:], bank[0:64, :], 0.0, 2.0, ALU.is_ge, ALU.mult).then_inc(gate_step, 1)
                    nc.vector.tensor_scalar(g_rows[:], bank[0:64, :], -1.0, GATE_MIN, ALU.mult, ALU.max).then_inc(gate_step, 1)
                    dve.wait_ge(gate_step, 2)
                    nc.vector.tensor_tensor(g_rows[:], bank[0:64, :], g_rows[:], ALU.max).then_inc(gate_step, 1)
                    dve.wait_ge(gate_step, 3)
                    nc.vector.scalar_tensor_tensor(g_rows[:], g_sign[:], -1.0, g_rows[:], ALU.add, ALU.mult).then_inc(gate_step, 1)
                elif e[0] == "ln":
                    _, which, b, t = e
                    n = NTH[e]
                    k = n % NXN
                    if which == 1:
                        dve.wait_ge(got_x[b], 16)
                    else:
                        dve.wait_ge(x2_ready, NT * b + t + 1)
                    if n >= NXN:
                        dve.wait_ge(xn_ready, n - NXN + 1)
                    nc.vector.bn_stats(st6[:, k], x_sb[:, b, t]).then_inc(bn_done, 1)
                    dve.wait_ge(bn_done, n + 1)
                    nc.vector.bn_aggr(mv[:, k], st6[:, k]).then_inc(mv_ready, 1)
                    dve.wait_ge(mv_ready, n + 1)
                    nc.vector.tensor_scalar(var_eps[:, k:k + 1], mv[:, k, 1:2], EPS, None, ALU.add).then_inc(veps_ready, 1)
                elif e[0] == "xn":
                    _, which, b, t = e
                    n = NTH[e]
                    k = n % NXN
                    dve.wait_ge(rstd_ready, n + 1)
                    nc.vector.tensor_scalar(xn[:, k], x_sb[:, b, t], mv[:, k, 0:1], rstd[:, k:k + 1],
                                            ALU.subtract, ALU.mult).then_inc(xn_ready, 1)
                elif e[0] == "tr":
                    _, which, b, t = e
                    dve.wait_ge(full, n2 + 1)
                    dve.wait_ge(mod_ready, 2 * which)
                    if which == 1 and b >= 1:
                        dve.wait_ge(v_ready, 2 * b)
                    if which == 2 and b >= 1:
                        dve.wait_ge(a_ready, NTH[("up", b - 1, t, 1)] + 1)
                    for c in range(KC):
                        ins = nc.vector.tensor_scalar(h_t[which - 1][:, c, t * P:(t + 1) * P], bank[:, c * P:(c + 1) * P],
                                                      scale_sb[:, which - 1, c, b:b + 1], shift_sb[:, which - 1, c, b:b + 1],
                                                      ALU.mult, ALU.add)
                    ins.then_inc(h_ready[which - 1], 1)
                elif e[0] == "qk":
                    n = NTH[e]
                    w = 2 * S if e[2] < 2 else S
                    dve.wait_ge(raw_ready, n + 1)
                    dve.wait_ge(got["rope"], 16)
                    if n >= 2:
                        dve.wait_ge(low_ready, n - 1)
                    for lo in (0, P // 2):
                        src, dst = slice(lo, lo + P // 2), slice(P // 2 - lo, P - lo)
                        nc.vector.tensor_tensor(shuf[dst, n % 2, 0:w].rearrange("p (g s) -> p g s", s=S),
                                                raw[src, n % 2, 0:w].rearrange("p (g s) -> p g s", s=S),
                                                rope_sb[src, 1:2, :].to_broadcast([P // 2, w // S, S]), ALU.mult).then_inc(rsin_ready, 1)
                elif e[0] == "rot":
                    n = NTH[e]
                    w = 2 * S if e[2] < 2 else S
                    dve.wait_ge(rsin_ready, 2 * n + 2)
                    dve.wait_ge(rcos_ready, n + 1)
                    nc.vector.tensor_tensor(raw[:, n % 2, 0:w], raw[:, n % 2, 0:w], shuf[:, n % 2, 0:w], ALU.add).then_inc(rot_ready, 1)
                elif e[0] == "split":
                    n = NTH[e]
                    w = 2 * S if e[2] < 2 else S
                    dve.wait_ge(high_ready, n + 1)
                    dve.wait_ge(rot_ready, n + 1)
                    nc.vector.tensor_tensor(shuf[:, n % 2, 0:w], raw[:, n % 2, 0:w], pieces[:, n % 2, 0, 0:w],
                                            ALU.subtract).then_inc(rest_ready, 1)
                elif e[0] == "max":
                    _, b, s = e
                    n = NTH[e]
                    qt, part = MSTEPS[s]
                    kw = (qt + 1) * P
                    heads = 2 * 512 // kw
                    dve.wait_ge(max_full, n + 1)
                    if b >= 1 and part == 0:
                        dve.wait_ge(piece, 5 * (NT * (b - 1) + qt + 1))
                    nc.vector.reduce_max(mx[:, qt, part * heads:(part + 1) * heads],
                                         sc_ps[:, 2 * (s % 2):2 * (s % 2) + 2].rearrange("p b n -> p (b n)").rearrange("p (h k) -> p h k", k=kw),
                                         AX.X).then_inc(max_done, 1)
                elif e[0] == "neg":
                    _, b, qt = e
                    n = NTH[e]
                    dve.wait_ge(max_done, NM * b + (NM0 if qt == 0 else NM))
                    if b >= 1:
                        dve.wait_ge(mt_ready, n - 1)
                    rest = mx[:, qt]
                    for k in range(NPIECE):
                        if k:
                            nc.vector.tensor_tensor(mres[:, k - 1], rest, m3[:, qt, k - 1], ALU.add).then_inc(piece, 1)
                            dve.wait_ge(piece, 5 * n + 2 * k)
                            rest = mres[:, k - 1]
                        nc.vector.tensor_scalar(m3[:, qt, k], rest, -1.0, None, ALU.mult).then_inc(piece, 1)
                        dve.wait_ge(piece, 5 * n + 2 * k + 1)
                elif e[0] == "norm":
                    _, b, qt = e
                    n = NTH[e]
                    dve.wait_ge(pv_done, NU * b + LAST_PV[qt][1] + 1)
                    dve.wait_ge(kept, 2 * n + 2)
                    for c in range(2):
                        w, k = slice(c * 2 * P, (c + 1) * 2 * P), 8 * n + 4 * c
                        nc.vector.scalar_tensor_tensor(z_sb[:, w], pv_ps[1][:, w], halves_sb[:, 0:1], z_sb[:, w],
                                                       ALU.mult, ALU.add).then_inc(norm_step, 1)
                        nc.vector.scalar_tensor_tensor(o_sb[:, n % 2, w], pv_ps[1][:, w], halves_sb[:, 1:2], o_sb[:, n % 2, w],
                                                       ALU.mult, ALU.add).then_inc(norm_step, 1)
                        dve.wait_ge(norm_step, k + 1)
                        nc.vector.reciprocal(z_sb[:, w], z_sb[:, w]).then_inc(norm_step, 1)
                        dve.wait_ge(norm_step, k + 3)
                        nc.vector.stream_shuffle(z_sb[:, w], z_sb[:, w], SWAP).then_inc(norm_step, 1)
                        dve.wait_ge(norm_step, k + 4)
                        nc.vector.tensor_tensor(o_sb[:, n % 2, w], o_sb[:, n % 2, w], z_sb[:, w], ALU.mult).then_inc(o_ready, 1)
                elif e[0] == "osplit":
                    n = NTH[e]
                    for c in range(2):
                        dve.wait_ge(o_hi_ready, 2 * n + 1 + c)
                        w = slice(c * 2 * P, (c + 1) * 2 * P)
                        nc.vector.tensor_tensor(o_lo[:, n % 2, w], o_sb[:, n % 2, w], o_hi[:, n % 2, w].bitcast(F32),
                                                ALU.subtract).then_inc(o_lo_ready, 1)
                elif e[0] == "asplit":
                    _, b, t = e
                    dve.wait_ge(a_hi_ready, NTH[e] + 1)
                    w = slice(t * P, (t + 1) * P)
                    nc.vector.tensor_tensor(a_lo[:, :, w], a_t[:, :, w], a_hi[:, :, w].bitcast(F32), ALU.subtract).then_inc(a_lo_ready, 1)
                elif e[0] in ("wo", "down"):
                    _, b, t = e
                    n = ngated(e)
                    branch = 0 if e[0] == "wo" else 1
                    dve.wait_ge(full, n2 + 1)
                    dve.wait_ge(got_gate[branch], 16 * (b + 1))
                    if n >= 2:
                        dve.wait_ge(x2_ready, sum(1 for f in SCHEDULE if f[0] == "wo" and ngated(f) <= n - 2))
                        k = sum(1 for f in SCHEDULE if f[0] == "down" and ngated(f) <= n - 2)
                        if k:
                            dve.wait_ge(out_ready, k)
                    nc.vector.tensor_tensor(gated[:, n % 2], bank[:], gate_sb[:, branch], ALU.mult).then_inc(gated_ready, 1)
                elif e[0] == "up":
                    _, b, t, i = e
                    n = NTH[e]
                    dve.wait_ge(act_ready, n + 1)
                    if b >= 1:
                        dve.wait_ge(gated_ready, ngated(("down", b - 1, t)) + 1)
                    for m in range(2):
                        mc = 2 * i + m
                        ins = nc.vector.scalar_tensor_tensor(a_t[:, mc, t * P:(t + 1) * P], bank[:, S + m * P:S + (m + 1) * P],
                                                             b12_sb[:, MC + mc:MC + mc + 1], act_s[:, n % 2, m], ALU.add, ALU.mult)
                    ins.then_inc(a_ready, 1)

        @block.tensor
        def _(pe):
            def product(out, a_hi, a_lo, w_hi, w_lo, first, final):
                nc.tensor.matmul(out, a_hi, w_hi, start=first, stop=False)
                nc.tensor.matmul(out, a_hi, w_lo, start=False, stop=False)
                return nc.tensor.matmul(out, a_lo, w_hi, start=False, stop=final)

            for e in SCHEDULE:
                if e[0] in GEN_KINDS:
                    bank, full, n2 = gen(e)
                    if n2:
                        pe.wait_ge(*read_out(GEN_ORDER[GEN[e] - 2]))
                if e[0] == "mods":
                    i = e[1]
                    pe.wait_ge(silu_step, 3)
                    for k in range(KC):
                        pe.wait_ge(got_mod[i][k], 16)
                        for s in range(2):
                            last = nc.tensor.matmul(bank[32 * s:32 * s + 32, :], c_silu[:, k], wmod_sb[i][:, s, k],
                                                    start=(k == 0), stop=(k == KC - 1), skip_group_check=True)
                    last.then_inc(full, 1)
                elif e[0] == "modt":
                    i = e[1]
                    pe.wait_ge(mod_row, i + 1)
                    pe.wait_ge(got["ident"], 16)
                    for c in range(KC):
                        last = nc.tensor.transpose(bank[:, c * 64:(c + 1) * 64], modrow[:, i, c * P:(c + 1) * P], ident_sb[0:64, 0:64])
                    last.then_inc(full, 1)
                elif e[0] == "tr":
                    _, which, b, t = e
                    n = NTH[("xn", which, b, t)]
                    pe.wait_ge(xn_ready, n + 1)
                    pe.wait_ge(got["ident"], 16)
                    for c in range(KC):
                        last = nc.tensor.transpose(bank[:, c * P:(c + 1) * P], xn[:, n % NXN, c * P:(c + 1) * P], ident_sb[:])
                    last.then_inc(full, 1)
                elif e[0] == "qk":
                    _, b, i = e
                    pe.wait_ge(h_ready[0], NT * (b + 1))
                    h1 = h_t[0]
                    if i < 2:
                        pe.wait_ge(got["wq"], 16)
                        for g in (2 * i, 2 * i + 1):
                            for k in range(KC):
                                last = nc.tensor.matmul(bank[:, (g % 2) * S:(g % 2 + 1) * S], wq_sb[:, k, g], h1[:, k],
                                                        start=(k == 0), stop=(k == KC - 1))
                    else:
                        pe.wait_ge(got["wk"], 16)
                        pe.wait_ge(got["wv"], 16)
                        for k in range(KC):
                            nc.tensor.matmul(bank[:, 0:S], wk_sb[:, k], h1[:, k], start=(k == 0), stop=(k == KC - 1))
                        for t in range(NT):
                            for k in range(KC):
                                last = nc.tensor.matmul(bank[:, S + t * P:S + (t + 1) * P], h1[:, k, t * P:(t + 1) * P],
                                                        wv_sb[:, k], start=(k == 0), stop=(k == KC - 1))
                    last.then_inc(full, 1)
                elif e[0] == "max":
                    _, b, s = e
                    n = NTH[e]
                    qt, part = MSTEPS[s]
                    kw = (qt + 1) * P
                    per_bank = 512 // kw
                    if s == 0:
                        for i in range(3):
                            pe.wait_ge(*stacked(b, i))
                        pe.wait_ge(got["bf"], 32)
                    if s >= 2:
                        pe.wait_ge(max_done, n - 1)
                    elif b:
                        pe.wait_ge(exp_done, 2 * NU * b - 1 + s)
                    for k in range(2):
                        heads = sc_ps[:, 2 * (s % 2) + k].rearrange("p (h k) -> p h k", k=kw)
                        nc.tensor.matmul(heads[:, :, qt * P:kw], ident16_sb[:], mask16_sb[:].unsqueeze(1).to_broadcast([P, per_bank, P]),
                                         start=True, stop=False, skip_group_check=True)
                        for i in range(per_bank):
                            v, g = divmod((part * 2 + k) * per_bank + i, G)
                            last = nc.tensor.matmul(heads[:, i], q_st[b % 2][0:PR, v, g, qt * P:(qt + 1) * P],
                                                    k_st[0:PR, b % 2, v, 0:kw], start=False, stop=(i == per_bank - 1),
                                                    skip_group_check=True)
                    last.then_inc(max_full, 1)
                elif e[0] == "mt":
                    _, b, qt = e
                    n = NTH[e]
                    pe.wait_ge(piece, 5 * (n + 1))
                    pe.wait_ge(got["bf"], 32)
                    nc.tensor.transpose(bank[0:NPIECE * NV * G, :].bitcast(BF16)[:, 0:P],
                                        m3[:, qt].rearrange("p t h -> p (t h)"), ident16_sb[:]).then_inc(full, 1)
                elif e[0] == "st":
                    _, b, u = e
                    n = NTH[e]
                    qt, h, kt = UNITS[u]
                    if u == 0:
                        pe.wait_ge(zeroed, 4)
                    pe.wait_ge(m_stacked[qt], 16 * (b + 1))
                    for j in range(NJ):
                        if j % 2 == 0 and u == 0:
                            pe.wait_ge(max_done, NM * (b + 1) - 1 + j // 2)
                        elif j % 2 == 0:
                            pe.wait_ge(exp_done, 2 * n - 1 + j // 2)
                        v = 2 * j + h
                        last = nc.tensor.matmul(sc_ps[:, j].rearrange("p (g q) -> p g q", q=P), k_st[0:SR, b % 2, v, kt * P:(kt + 1) * P],
                                                q_st[b % 2][0:SR, v, :, qt * P:(qt + 1) * P], start=True, stop=True)
                        if j % 2 == 1:
                            last.then_inc(st_full, 1)
                elif e[0] == "pv":
                    _, b, u = e
                    n = NTH[e]
                    qt, h, kt = UNITS[u]
                    pe.wait_ge(exp_done, 2 * (n + 1))
                    if MASKED[u]:
                        pe.wait_ge(mask_done, nmasked(b, u))
                    first, final = kt == qt, kt == 0
                    before = NT * b + qt
                    if first and h == 0:
                        pe.wait_ge(v_ready, 2 * (b + 1))
                    if first and before:
                        if h == 0:
                            pe.wait_ge(kept, 2 * before)
                        else:
                            pe.wait_ge(norm_step, 8 * before - 2)
                    for j in range(NJ):
                        last = nc.tensor.matmul(pv_ps[h][32 * j:32 * j + 32, :], v1[:, b % 2, kt, h, j], probs[:, n % 3, j],
                                                start=first, stop=final, skip_group_check=True)
                    last.then_inc(pv_done, 1)
                elif e[0] == "wo":
                    _, b, qt = e
                    n = NTH[e]
                    pe.wait_ge(w_lo, 1)
                    for g in range(G):
                        if g % 2 == 0:
                            pe.wait_ge(o_lo_ready, 2 * n + 1 + g // 2)
                        last = product(bank[:], o_hi[:, n % 2, g * P:(g + 1) * P], o_lo[:, n % 2, g * P:(g + 1) * P],
                                       wo_hi[:, g], wo_lo[:, g], g == 0, g == G - 1)
                    last.then_inc(full, 1)
                elif e[0] == "up":
                    _, b, t, i = e
                    pe.wait_ge(h_ready[1], NT * b + t + 1)
                    pe.wait_ge(got["w12"], 16)
                    for s in range(2):
                        for m in range(2):
                            col = s * M + (2 * i + m) * P
                            for k in range(KC):
                                last = nc.tensor.matmul(bank[:, s * S + m * P:s * S + (m + 1) * P], w12_sb[:, k, col:col + P],
                                                        h_t[1][:, k, t * P:(t + 1) * P], start=(k == 0), stop=(k == KC - 1))
                    last.then_inc(full, 1)
                elif e[0] == "down":
                    _, b, t = e
                    pe.wait_ge(a_lo_ready, NTH[("asplit", b, t)] + 1)
                    pe.wait_ge(w_lo, 2)
                    for mc in range(MC):
                        w = slice(t * P, (t + 1) * P)
                        last = product(bank[:], a_hi[:, mc, w], a_lo[:, mc, w], w3_hi[:, mc], w3_lo[:, mc], mc == 0, mc == MC - 1)
                    last.then_inc(full, 1)


def constants():
    f = np.float32
    bf16 = mybir.dt.np(mybir.dt.bfloat16)
    inv_freq = f(1.0) / f(10000.0) ** (np.arange(0, DH, 2, dtype=f) / f(DH))
    freqs = np.arange(S, dtype=f)[:, None] * inv_freq[None, :]
    d = np.arange(P) // NV
    cos = np.cos(freqs)[:, d % (DH // 2)].T
    sin = np.sin(freqs)[:, d % (DH // 2)].T * np.where(d < DH // 2, f(1), f(-1))[:, None]
    rope = np.stack([cos, sin], 1).astype(f)
    row = np.arange(P)
    ident = np.eye(P, dtype=f)
    mask16 = np.where(row[None, :] > row[:, None], f(NEG), f(0)).astype(bf16)
    halves = np.stack([row % 32 < 16, row % 32 >= 16], 1).astype(f)
    return {"rope": rope, "halves": halves, "ident": ident, "ident16": ident.astype(bf16),
            "mask16": mask16}


def kernel(L0_attn_x, L0_attn_Wq, L0_attn_Wk, L0_attn_Wv, L0_attn_Wo, L0_ffn_w12, L0_ffn_b12, L0_ffn_w3, L0_ffn_b3,
           L0_c, L0_wmod):
    import concourse.bacc as bacc
    from concourse.bass_utils import run_bass_kernel_spmd

    def rows(a):
        a = np.asarray(a)
        return a.reshape(a.shape[0] // P, P, *a.shape[1:]).swapaxes(0, 1)

    arrays = {
        "x": np.asarray(L0_attn_x).reshape(B, NT, P, D).transpose(0, 2, 1, 3),
        "c_t": rows(np.asarray(L0_c).T),
        "wmod": rows(np.asarray(L0_wmod).reshape(D, 6, D)[:, [0, 1, 3, 4, 2, 5]]).transpose(0, 2, 1, 3),
        "wq": rows(np.asarray(L0_attn_Wq).reshape(D, NH, NJ, G, DH).transpose(0, 3, 4, 2, 1).reshape(D, G, P)),
        "wk": rows(np.asarray(L0_attn_Wk).reshape(D, NH, NJ, DH).transpose(0, 3, 2, 1).reshape(D, P)),
        "wv": rows(np.asarray(L0_attn_Wv)),
        "wo": np.asarray(L0_attn_Wo).reshape(NH, NJ, G, DH, D).transpose(1, 0, 3, 2, 4).reshape(P, G, D),
        "w12": rows(np.asarray(L0_ffn_w12).T),
        "w3": rows(np.asarray(L0_ffn_w3).T),
        "b12": np.asarray(L0_ffn_b12).reshape(2 * MC, P).T,
        "b3": np.asarray(L0_ffn_b3).reshape(D),
        **constants(),
    }
    arrays = {k: np.ascontiguousarray(v) for k, v in arrays.items()}
    nc = bacc.Bacc("TRN2", target_bir_lowering=False, num_devices=1)
    aps = {k: nc.dram_tensor(f"in_{k}", v.shape, mybir.dt.from_np(v.dtype), kind="ExternalInput").ap() for k, v in arrays.items()}
    out = nc.dram_tensor("out", (B, NT, P, D), mybir.dt.float32, kind="ExternalOutput").ap()
    build(nc, out=out, **aps)
    r = run_bass_kernel_spmd(nc, [{f"in_{k}": v for k, v in arrays.items()}], core_ids=[0])
    return r.results[0]["out"].reshape(B, S, D)
```
